# Optimizing a Trainium2 kernel written in Bass

```python
import numpy as np
import jax
import jax.numpy as jnp

def _softmax(x, axis=-1):
    return jax.nn.softmax(x, axis=axis)

def _gelu(x):
    return jax.nn.gelu(x, approximate=True)

def _silu(x):
    return jax.nn.silu(x)

def _sigmoid(x):
    return jax.nn.sigmoid(x)

def _layernorm(x, axis=-1, eps=1e-05):
    m = jnp.mean(x, axis=axis, keepdims=True)
    v = jnp.var(x, axis=axis, keepdims=True)
    return (x - m) / jnp.sqrt(v + eps)

def _scatter_add(tgt, idx, src, axis=0):
    return tgt.at[idx].add(src)

def _segment_sum(src, seg, n):
    return jax.ops.segment_sum(src, seg, n)
kernel_name = 'mk_adaln_d2_jaxref_r8_bea24f'

def setup_inputs(seed: int=0):
    np.random.seed(seed)
    _w = jnp.asarray

    def _L0_attn_setup():
        import jax, jax.numpy as jnp
        import numpy as np
        EMBED = 128
        N_HEAD = 16
        HEAD_DIM = EMBED // N_HEAD
        key = jax.random.key(seed)
        ks = jax.random.split(key, 9)

        def xavier(k, shape, fan_in, fan_out):
            bound = float(np.sqrt(6.0 / (fan_in + fan_out)))
            return jax.random.uniform(k, shape, jnp.float32, -bound, bound)
        x = jax.random.normal(ks[0], (4, 256, EMBED), jnp.float32)
        wq = xavier(ks[1], (N_HEAD, EMBED, HEAD_DIM), EMBED, HEAD_DIM)
        wk = xavier(ks[2], (N_HEAD, EMBED, HEAD_DIM), EMBED, HEAD_DIM)
        wv = xavier(ks[3], (N_HEAD, EMBED, HEAD_DIM), EMBED, HEAD_DIM)
        bq = jnp.zeros((N_HEAD, 1, HEAD_DIM), jnp.float32)
        bk = jnp.zeros((N_HEAD, 1, HEAD_DIM), jnp.float32)
        bv = jnp.zeros((N_HEAD, 1, HEAD_DIM), jnp.float32)
        bnd = 1.0 / float(np.sqrt(EMBED))
        wo = jax.random.uniform(ks[4], (EMBED, EMBED), jnp.float32, -bnd, bnd)
        bo = jax.random.uniform(ks[5], (EMBED,), jnp.float32, -bnd, bnd)
        return {'x': x, 'wq': wq, 'bq': bq, 'wk': wk, 'bk': bk, 'wv': wv, 'bv': bv, 'wo': wo, 'bo': bo}
    _L0_attn_in = _L0_attn_setup()

    def _L0_ffn_setup():
        import jax, jax.numpy as jnp
        import numpy as np
        NUM_EXPERTS = 8
        EXPERT_CAPACITY = 2.0
        DIM = 128
        HIDDEN_DIM = 512
        key = jax.random.key(seed)
        k_x, k_g, k_w1, k_w2 = jax.random.split(key, 4)
        n, t, d, f, e = (8, 128, DIM, HIDDEN_DIM, NUM_EXPERTS)
        x = jax.random.normal(k_x, (n, t, d), dtype=jnp.float32)
        gate_w = jax.random.normal(k_g, (e, d), dtype=jnp.float32) * 0.02
        w1 = jax.random.normal(k_w1, (e, d, f), dtype=jnp.float32) * 0.02
        w2 = jax.random.normal(k_w2, (e, f, d), dtype=jnp.float32) * 0.02
        return {'x': x, 'gate_w': gate_w, 'w1': w1, 'w2': w2}
    _L0_ffn_in = _L0_ffn_setup()
    _L0_c = _w((lambda *s: np.random.randn(*s).astype(np.float32) * 0.05)(8, 128))
    _L0_wmod = _w((lambda *s: np.random.randn(*s).astype(np.float32) * 0.05)(128, 6 * 128) * 128 ** (-0.5))

    def _L1_attn_setup():
        import jax, jax.numpy as jnp
        import numpy as np
        B, T, D, H, R = (4, 512, 128, 16, 32)
        DH = D // H
        key = jax.random.key(seed)
        ks = jax.random.split(key, 5)
        s = 0.02
        return {'x': jax.random.normal(ks[0], (B, T, D), dtype=jnp.float32), 'Wq': jax.random.normal(ks[1], (D, D), dtype=jnp.float32) * s, 'bq': jnp.zeros((D,), dtype=jnp.float32), 'Wd': jax.random.normal(ks[2], (D, R), dtype=jnp.float32) * s, 'bd': jnp.zeros((R,), dtype=jnp.float32), 'Wu': jax.random.normal(ks[3], (R, 2 * D), dtype=jnp.float32) * s, 'bu': jnp.zeros((2 * D,), dtype=jnp.float32), 'Wo': jax.random.normal(ks[4], (D, D), dtype=jnp.float32) * s, 'bo': jnp.zeros((D,), dtype=jnp.float32)}
    _L1_attn_in = _L1_attn_setup()

    def _L1_ffn_setup():
        import jax, jax.numpy as jnp
        import numpy as np
        B, S, D, E, H, DO = (4, 256, 128, 8, 512, 128)
        TOP_K = 2
        LN_EPS = 1e-05
        key = jax.random.key(seed)
        ks = jax.random.split(key, 9)
        s = 0.02
        return {'x': jax.random.normal(ks[0], (B, S, D), dtype=jnp.float32), 'W1': jax.random.normal(ks[1], (E, D, H), dtype=jnp.float32) * s, 'b1': jnp.zeros((E, H), dtype=jnp.float32), 'W2': jax.random.normal(ks[2], (E, H, DO), dtype=jnp.float32) * s, 'b2': jnp.zeros((E, DO), dtype=jnp.float32), 'gate_W': jax.random.normal(ks[3], (D, E), dtype=jnp.float32) * s, 'shared_W': jax.random.normal(ks[4], (D, DO), dtype=jnp.float32) * s, 'shared_b': jnp.zeros((DO,), dtype=jnp.float32), 'gamma': jnp.ones((DO,), dtype=jnp.float32), 'beta': jnp.zeros((DO,), dtype=jnp.float32)}
    _L1_ffn_in = _L1_ffn_setup()
    _L1_c = _w((lambda *s: np.random.randn(*s).astype(np.float32) * 0.05)(8, 128))
    _L1_wmod = _w((lambda *s: np.random.randn(*s).astype(np.float32) * 0.05)(128, 6 * 128) * 128 ** (-0.5))
    _d = {'L0_attn_x': _L0_attn_in['x'], 'L0_attn_wq': _L0_attn_in['wq'], 'L0_attn_bq': _L0_attn_in['bq'], 'L0_attn_wk': _L0_attn_in['wk'], 'L0_attn_bk': _L0_attn_in['bk'], 'L0_attn_wv': _L0_attn_in['wv'], 'L0_attn_bv': _L0_attn_in['bv'], 'L0_attn_wo': _L0_attn_in['wo'], 'L0_attn_bo': _L0_attn_in['bo'], 'L0_ffn_gate_w': _L0_ffn_in['gate_w'], 'L0_ffn_w1': _L0_ffn_in['w1'], 'L0_ffn_w2': _L0_ffn_in['w2'], 'L0_c': _L0_c, 'L0_wmod': _L0_wmod, 'L1_attn_Wq': _L1_attn_in['Wq'], 'L1_attn_bq': _L1_attn_in['bq'], 'L1_attn_Wd': _L1_attn_in['Wd'], 'L1_attn_bd': _L1_attn_in['bd'], 'L1_attn_Wu': _L1_attn_in['Wu'], 'L1_attn_bu': _L1_attn_in['bu'], 'L1_attn_Wo': _L1_attn_in['Wo'], 'L1_attn_bo': _L1_attn_in['bo'], 'L1_ffn_W1': _L1_ffn_in['W1'], 'L1_ffn_b1': _L1_ffn_in['b1'], 'L1_ffn_W2': _L1_ffn_in['W2'], 'L1_ffn_b2': _L1_ffn_in['b2'], 'L1_ffn_gate_W': _L1_ffn_in['gate_W'], 'L1_ffn_shared_W': _L1_ffn_in['shared_W'], 'L1_ffn_shared_b': _L1_ffn_in['shared_b'], 'L1_ffn_gamma': _L1_ffn_in['gamma'], 'L1_ffn_beta': _L1_ffn_in['beta'], 'L1_c': _L1_c, 'L1_wmod': _L1_wmod}
    _x0 = _d['L0_attn_x']
    _d['L0_attn_x'] = jax.random.normal(jax.random.fold_in(jax.random.key(seed), 1), (8, 512, 128), dtype=_x0.dtype)
    del _x0
    return _d

def reference(L0_attn_x, L0_attn_wq, L0_attn_bq, L0_attn_wk, L0_attn_bk, L0_attn_wv, L0_attn_bv, L0_attn_wo, L0_attn_bo, L0_ffn_gate_w, L0_ffn_w1, L0_ffn_w2, L0_c, L0_wmod, L1_attn_Wq, L1_attn_bq, L1_attn_Wd, L1_attn_bd, L1_attn_Wu, L1_attn_bu, L1_attn_Wo, L1_attn_bo, L1_ffn_W1, L1_ffn_b1, L1_ffn_W2, L1_ffn_b2, L1_ffn_gate_W, L1_ffn_shared_W, L1_ffn_shared_b, L1_ffn_gamma, L1_ffn_beta, L1_c, L1_wmod):

    def _L0_attn_ref(x, wq, bq, wk, bk, wv, bv, wo, bo):
        import jax, jax.numpy as jnp
        import numpy as np
        EMBED = 128
        N_HEAD = 16
        HEAD_DIM = EMBED // N_HEAD
        q = jnp.einsum('bsd,hde->bhse', x, wq) + bq
        k = jnp.einsum('bsd,hde->bhse', x, wk) + bk
        v = jnp.einsum('bsd,hde->bhse', x, wv) + bv
        scale = 1.0 / jnp.sqrt(jnp.asarray(q.shape[-1], q.dtype))
        scores = jax.nn.softmax(jnp.einsum('bhse,bhte->bhst', q, k) * scale, axis=-1)
        att = jnp.einsum('bhst,bhte->bhse', scores, v)
        b, h, s, e = att.shape
        att = att.transpose(0, 2, 1, 3).reshape(b, s, h * e)
        return att @ wo.T + bo

    def _L0_ffn_ref(x, gate_w, w1, w2):
        import jax, jax.numpy as jnp
        import numpy as np
        NUM_EXPERTS = 8
        EXPERT_CAPACITY = 2.0
        DIM = 128
        HIDDEN_DIM = 512
        n, t, d = x.shape
        e = gate_w.shape[0]
        k = int(EXPERT_CAPACITY * t / e)
        scores = jnp.einsum('ntd,ed->nte', x, gate_w)
        probs = jax.nn.softmax(scores, axis=-1)
        g, m = jax.lax.top_k(probs.transpose(0, 2, 1), k)
        batch_idx = jnp.arange(n)[:, None, None]
        xin = x[batch_idx, m]
        h = jnp.einsum('nekd,edf->nekf', xin, w1)
        h = jax.nn.gelu(h, approximate=False)
        h = jnp.einsum('nekf,efd->nekd', h, w2)
        out_tok = g[..., None] * h
        out = jnp.zeros((n, t, d), dtype=x.dtype).at[batch_idx, m].add(out_tok)
        return out

    def _L1_attn_ref(x, Wq, bq, Wd, bd, Wu, bu, Wo, bo):
        import jax, jax.numpy as jnp
        import numpy as np
        B, T, D, H, R = (4, 512, 128, 16, 32)
        DH = D // H
        b, t = (x.shape[0], x.shape[1])
        q = (x @ Wq + bq).reshape(b, t, H, DH)
        kv = ((x @ Wd + bd) @ Wu + bu).reshape(b, t, H, 2 * DH)
        k, v = (kv[..., :DH], kv[..., DH:])
        q = jax.nn.elu(q) + 1.0
        k = jax.nn.elu(k) + 1.0
        context = jnp.einsum('bthd,bthe->bhde', k, v)
        out = jnp.einsum('bthd,bhde->bthe', q, context)
        k_sum = k.sum(axis=1)
        z = 1.0 / (jnp.einsum('bthd,bhd->bth', q, k_sum) + 1e-06)
        out = out * z[..., None]
        return out.reshape(b, t, D) @ Wo + bo

    def _L1_ffn_ref(x, W1, b1, W2, b2, gate_W, shared_W, shared_b, gamma, beta):
        import jax, jax.numpy as jnp
        import numpy as np
        B, S, D, E, H, DO = (4, 256, 128, 8, 512, 128)
        TOP_K = 2
        LN_EPS = 1e-05
        d = x.shape[-1]
        flat = x.reshape(-1, d)
        n_exp = gate_W.shape[-1]
        probs = jax.nn.softmax(flat @ gate_W, axis=-1)
        topk_w, topk_idx = jax.lax.top_k(probs, TOP_K)
        topk_w = topk_w / topk_w.sum(axis=-1, keepdims=True)
        combine = (jax.nn.one_hot(topk_idx, n_exp, dtype=flat.dtype) * topk_w[..., None]).sum(axis=1)
        out = 0.5 * jax.nn.gelu(flat @ shared_W + shared_b, approximate=False)
        for e in range(n_exp):
            h = jax.nn.gelu(flat @ W1[e] + b1[e], approximate=False)
            out = out + combine[:, e:e + 1] * (h @ W2[e] + b2[e])
        mean = out.mean(axis=-1, keepdims=True)
        var = ((out - mean) ** 2).mean(axis=-1, keepdims=True)
        out = (out - mean) * jax.lax.rsqrt(var + LN_EPS) * gamma + beta
        return out.reshape(*x.shape[:-1], out.shape[-1])
    x = L0_attn_x
    mod = (_silu(L0_c) @ L0_wmod).reshape(L0_c.shape[0], 6, 1, -1)
    sa, ca, ga, sb, cb, gb = (mod[:, 0], mod[:, 1], mod[:, 2], mod[:, 3], mod[:, 4], mod[:, 5])
    ga = (2 * (ga >= 0) - 1) * jnp.maximum(jnp.abs(ga), 0.25)
    gb = (2 * (gb >= 0) - 1) * jnp.maximum(jnp.abs(gb), 0.25)
    h = _layernorm(x, axis=-1) * (1 + ca) + sa
    x = x + ga * _L0_attn_ref(h, L0_attn_wq, L0_attn_bq, L0_attn_wk, L0_attn_bk, L0_attn_wv, L0_attn_bv, L0_attn_wo, L0_attn_bo)
    h = _layernorm(x, axis=-1) * (1 + cb) + sb
    x = x + gb * _L0_ffn_ref(h, L0_ffn_gate_w, L0_ffn_w1, L0_ffn_w2)
    mod = (_silu(L1_c) @ L1_wmod).reshape(L1_c.shape[0], 6, 1, -1)
    sa, ca, ga, sb, cb, gb = (mod[:, 0], mod[:, 1], mod[:, 2], mod[:, 3], mod[:, 4], mod[:, 5])
    ga = (2 * (ga >= 0) - 1) * jnp.maximum(jnp.abs(ga), 0.25)
    gb = (2 * (gb >= 0) - 1) * jnp.maximum(jnp.abs(gb), 0.25)
    h = _layernorm(x, axis=-1) * (1 + ca) + sa
    x = x + ga * _L1_attn_ref(h, L1_attn_Wq, L1_attn_bq, L1_attn_Wd, L1_attn_bd, L1_attn_Wu, L1_attn_bu, L1_attn_Wo, L1_attn_bo)
    h = _layernorm(x, axis=-1) * (1 + cb) + sb
    x = x + gb * _L1_ffn_ref(h, L1_ffn_W1, L1_ffn_b1, L1_ffn_W2, L1_ffn_b2, L1_ffn_gate_W, L1_ffn_shared_W, L1_ffn_shared_b, L1_ffn_gamma, L1_ffn_beta)
    return x

_drawn_inputs = setup_inputs


def setup_inputs(seed=0):
    import zlib

    import numpy as np

    out = dict(_drawn_inputs(seed))
    spreads = {'L0_attn_bq': (0.0, 0.615),
     'L0_attn_bk': (0.0, 0.8),
     'L0_attn_bv': (0.0, 0.329),
     'L1_attn_bq': (0.0, 0.8),
     'L1_attn_bd': (0.0, 0.8),
     'L1_attn_bu': (0.0, 0.408),
     'L1_attn_bo': (0.0, 0.1),
     'L1_ffn_b1': (0.0, 0.1),
     'L1_ffn_b2': (0.0, 0.1),
     'L1_ffn_shared_b': (0.0, 0.1),
     'L1_ffn_gamma': (1.0, 0.2),
     'L1_ffn_beta': (0.0, 0.334)}
    factors = {'L0_ffn_gate_w': 6.742,
     'L0_ffn_w1': 6.314,
     'L0_ffn_w2': 6.647,
     'L1_attn_Wq': 8.0,
     'L1_attn_Wd': 8.0,
     'L1_attn_Wu': 8.0,
     'L1_attn_Wo': 3.871}
    for name, (base, spread) in spreads.items():
        noise = np.random.default_rng([zlib.crc32(name.encode()), seed]).standard_normal(out[name].shape)
        drawn = base * np.exp(spread * noise) if base else spread * noise
        out[name] = jnp.asarray(drawn.astype(out[name].dtype))
    for name, factor in factors.items():
        out[name] = (out[name] * factor).astype(out[name].dtype)
    return out
```

```python
from contextlib import ExitStack

import concourse.bass as bass
from concourse import mybir

F32 = mybir.dt.float32
BF16 = mybir.dt.bfloat16
F32R = mybir.dt.float32r
ALU = mybir.AluOpType
ACT = mybir.ActivationFunctionType
AX = mybir.AxisListType

P = 128
B, T, D = 8, 512, 128
NT = T // P
H, HD = 16, 8
HG = 4
NG = H // HG
E, F = 8, 512
NF = F // P
KSEL = 2 * T // E
EPS = 1e-5
UNITS = H * NT
PARTS = 3
TERMS = PARTS * PARTS
STACK = TERMS * HD
MROW = STACK
R = 32
QSLOTS = 5

SHIFT_A, SCALE_A, GATE_A, SHIFT_B, SCALE_B, GATE_B = range(6)


class Batch:

    def __init__(self, own, before=True, here=True, after=True):
        self.own, self.before, self.here, self.after = own, before, here, after


def as_bf16(bank):
    return bank[:].bitcast(BF16)


def window(tensor, offset, dims):
    return bass.AP(tensor=tensor, offset=offset, ap=dims)


def settle(eng):
    eng.nop(nofuse=True)


def norm(nc, half, xin, mv, rstd, step, bb, out, ready):
    pool = nc.gpsimd

    def over_features(ap):
        return ap.unsqueeze(2).to_broadcast([P, NT, D])

    settle(pool)
    nc.gpsimd.tensor_scalar(rstd[:, 0, :], mv[:, :, 1], EPS, None, ALU.add).then_inc(step, 1)
    nc.gpsimd.tensor_tensor(out[:], xin, over_features(mv[:, :, 0]), ALU.subtract).then_inc(step, 1)
    pool.wait_ge(step, 3 * bb + 1)
    nc.gpsimd.tensor_tensor(rstd[:, 1, :], rstd[:, 0, :], half[:], ALU.pow).then_inc(step, 1)
    pool.wait_ge(step, 3 * bb + 3)
    nc.gpsimd.tensor_tensor(out[:], out[:], over_features(rstd[:, 1, :]), ALU.mult).then_inc(ready, 1)


def scores_of(u, it):
    j = u // (HG * NT)
    if j < NG // 2:
        return it.own, j + NG // 2, it.here
    return it.own + 1, j - NG // 2, it.after


def program_attention(nc, io, keep, scratch, held):
    ctx = ExitStack()
    with ctx:
        def sb(name, shape, dt=F32):
            return ctx.enter_context(nc.sbuf_tensor(name, shape, dt))

        def pb(name, shape, dt=F32):
            return ctx.enter_context(nc.psum_tensor(name, shape, dt))

        def sem(name):
            held.append(nc.alloc_semaphore(name=name))
            return held[-1]

        x_all, probs_tok, mod, scale1, ident = (
            keep["x"], keep["probs"], keep["mod"], keep["scale1"], keep["ident"])

        wq = sb("wq", [P, P])
        wk = sb("wk", [P, P])
        wv = sb("wv", [P, P])
        wo = sb("wo", [P, P])
        bq = sb("bq", [P, 1])
        bk = sb("bk", [P, 1])
        bv = sb("bv", [P, P])
        gate_w = sb("gate_w", [P, E])
        wmod = sb("wmod", [P, 2, 6 * D])
        gates = sb("gates", [P, 2, B, D])
        cT = sb("cT", [P, 2, B])
        siluT = sb("siluT", [P, 2, B])
        sig = sb("sig", [P, 2, B])
        vectors = sb("vectors", [B, 4, D])
        gsign = sb("gsign", [B, 4, D])
        graw = sb("graw", [B, 4, D])
        gstep = sb("gstep", [B, 4, D])
        gabs = sb("gabs", [B, 4, D])
        gclamp = sb("gclamp", [B, 4, D])
        grow = sb("grow", [B, 7, D])
        ident_b = sb("ident_b", [P, P], BF16)
        ones = sb("ones", [48, T], BF16)
        half = sb("half", [P, NT])
        q_stack = [sb(f"q_stack{i}", [P, H, T], BF16) for i in range(2)]
        k_stack = [sb(f"k_stack{i}", [P, H, T], BF16) for i in range(2)]
        v_ext = [sb(f"v_ext{i}", [P, NT, H, 32]) for i in range(2)]
        probs = sb("p_ring", [P, 8, T])
        hT = sb("hT", [P, T])
        xh1 = sb("xh1", [P, NT, D])
        xh2 = sb("xh2", [P, NT, D])
        st1 = sb("st1", [P, NT, 6])
        mv1 = sb("mv1", [P, NT, 2])
        st2 = sb("st2", [P, NT, 6])
        mv2 = sb("mv2", [P, NT, 2])
        rstd1 = sb("rstd1", [P, 3, NT])
        rstd2 = sb("rstd2", [P, 3, NT])
        q_parts = sb("q_parts", [P, PARTS, T], BF16)
        k_parts = sb("k_parts", [P, PARTS, T], BF16)
        q_rest = sb("q_rest", [P, T])
        k_rest = sb("k_rest", [P, T])
        nmax = sb("nmax", [P, NG, HG * NT])
        m_rest = sb("m_rest", [P, HG * NT])
        m_parts = sb("m_parts", [P, NG, PARTS * HG * NT], BF16)
        m_rows = sb("m_rows", [PARTS * HG * NT, NG, P], BF16)
        att = sb("att", [P, 2, T])
        rec = sb("rec", [P, NG, NT, HG])
        att_tok = sb("att_tok", [P, NT, D])
        attT = sb("attT", [P, T])
        wo_gated = sb("wo_gated", [P, D])
        h2T = sb("h2T", [P, T])
        lg_max = sb("lg_max", [P, NT])
        lg = sb("lg", [P, NT, E])
        lg_exp = sb("lg_exp", [P, NT, E])
        lg_sum = sb("lg_sum", [P, NT])
        lg_inv = sb("lg_inv", [P, NT])
        prob_now = sb("prob_now", [P, NT, E])
        probT = sb("probT", [E, T])

        ps_s = [pb(f"ps_s{i}", [P, T]) for i in range(2)]
        ps_t = [pb(f"ps_t{i}", [P, T]) for i in range(3)]
        ps_av = pb("ps_av", [P, T])
        bank_a = pb("bank_a", [P, T])
        bank_b = pb("bank_b", [P, T])

        c_in = sem("c_in")
        wqkv_in = sem("wqkv_in")
        x0_in = sem("x0_in")
        x_in = sem("x_in")
        rest_in = sem("rest_in")
        ones_in = sem("ones_in")
        sig_e = sem("sig_e")
        silu = sem("silu")
        mod_mm = sem("mod_mm")
        mod_ready = sem("mod_ready")
        gate_mm = sem("gate_mm")
        gate_step = sem("gate_step")
        grow_ready = sem("grow_ready")
        grow_out = sem("grow_out")
        gates_in = sem("gates_in")
        consts = sem("consts")
        identb_ready = sem("identb_ready")
        st1_done = sem("st1_done")
        mv1_done = sem("mv1_done")
        r1_step = sem("r1_step")
        xh1_ready = sem("xh1_ready")
        hT_filled = sem("hT_filled")
        hT_ready = sem("hT_ready")
        q_filled = sem("q_filled")
        q1_ready = sem("q1_ready")
        q_rest_ready = sem("q_rest_ready")
        q2_ready = sem("q2_ready")
        q3_ready = sem("q3_ready")
        k_filled = sem("k_filled")
        k1_ready = sem("k1_ready")
        k_rest_ready = sem("k_rest_ready")
        k2_ready = sem("k2_ready")
        k3_ready = sem("k3_ready")
        v_filled = sem("v_filled")
        v_ready = sem("v_ready")
        q_saved = sem("q_saved")
        k_saved = sem("k_saved")
        stack_in = [sem(f"stack_in{j}") for j in range(NG)]
        s_filled = sem("s_filled")
        max_done = sem("max_done")
        t_filled = sem("t_filled")
        exp_done = sem("exp_done")
        av_done = sem("av_done")
        av_saved = sem("av_saved")
        m_step = sem("m_step")
        m_parts_ready = [sem(f"m_parts_ready{j}") for j in range(NG)]
        m_filled = [sem(f"m_filled{j}") for j in range(NG)]
        m_rows_ready = [sem(f"m_rows_ready{j}") for j in range(NG)]
        m_in = [sem(f"m_in{j}") for j in range(NG)]
        avT_filled = [sem(f"avT_filled{j}") for j in range(NG)]
        rec_done = [sem(f"rec_done{j}") for j in range(NG)]
        avT_read = [sem(f"avT_read{j}") for j in range(NG)]
        attT_filled = sem("attT_filled")
        attT_ready = sem("attT_ready")
        wog_ready = sem("wog_ready")
        xbias_ready = sem("xbias_ready")
        o_filled = sem("o_filled")
        x_ready = sem("x_ready")
        st2_done = sem("st2_done")
        mv2_done = sem("mv2_done")
        r2_step = sem("r2_step")
        xh2_ready = sem("xh2_ready")
        h2T_filled = sem("h2T_filled")
        h2T_ready = sem("h2T_ready")
        lg_filled = sem("lg_filled")
        lg_step = sem("lg_step")
        lg_ready = sem("lg_ready")
        lg_exp_ready = sem("lg_exp_ready")
        prob_inv = sem("prob_inv")
        prob_ready = sem("prob_ready")
        prob_kept = sem("prob_kept")
        pT_filled = sem("pT_filled")
        probT_ready = sem("probT_ready")
        probT_out = sem("probT_out")

        block = ctx.enter_context(nc.Block())

        def pipeline(eng, iteration):
            iteration(Batch(-1, before=False, here=False), 1)
            iteration(Batch(0, before=False), 0)
            iteration(Batch(1), 1)
            with eng.Fori(0, (B - 4) // 2) as i:
                iteration(Batch(2 * i + 2), 0)
                iteration(Batch(2 * i + 3), 1)
            iteration(Batch(B - 2), B % 2)
            iteration(Batch(B - 1, after=False), (B - 1) % 2)
            iteration(Batch(B, here=False, after=False), B % 2)

        def tokens(ap):
            return ap.rearrange("p (t n) -> p t n", t=NT)

        @block.sync
        def _(sp):
            sp.dma_start(cT[:], io["cT"]).then_inc(c_in, 16)
            sp.dma_start(x_all[:, 0], io["x"][0].rearrange("(t p) d -> p t d", p=P)).then_inc(x0_in, 16)
            sp.dma_start(wmod[:], io["wmod"]).then_inc(c_in, 16)
            sp.dma_start(ident[:], io["ident"]).then_inc(c_in, 16)
            for tile, name in ((wq, "wq"), (wk, "wk"), (wv, "wv"), (bq, "bq"), (bk, "bk")):
                sp.dma_start(tile[:], io[name]).then_inc(wqkv_in, 16)
            sp.dma_start(bv[:], io["bv"].partition_broadcast(P)).then_inc(wqkv_in, 16)
            sp.dma_start(vectors[:], io["vectors"].partition_broadcast(B)).then_inc(rest_in, 16)
            sp.dma_start(wo[:], io["wo"]).then_inc(rest_in, 16)
            sp.dma_start(gate_w[:], io["gate_w"]).then_inc(rest_in, 16)
            sp.dma_start(x_all[:, 1:B], io["x"][1:B].rearrange("b (t p) d -> p b t d", p=P)).then_inc(x_in, 16)
            sp.wait_ge(consts, 1)
            for i in range(2):
                sp.dma_start(k_stack[i][MROW:MROW + PARTS], ones[:]).then_inc(ones_in, 16)

            def move_maxima(bb, j, par):
                sp.wait_ge(m_rows_ready[j], bb + 1)
                sp.dma_start(q_stack[par][MROW:MROW + PARTS, HG * j:HG * (j + 1), :],
                             m_rows[:, j, :]).then_inc(m_in[j], 16)

            def save_parts(parts, ready, saved, dram, slots, bb):
                for j in range(NG):
                    sp.wait_ge(stack_in[j], 32 * bb)
                    settle(sp)
                for c in range(PARTS):
                    sp.wait_ge(ready[c], bb + 1)
                    for slot in range(c, slots, PARTS):
                        sp.dma_start(dram.ap()[slot * HD:(slot + 1) * HD].rearrange("e h t -> h e t"),
                                     parts[:, c, :]).then_inc(saved, 16)

            def iteration(it, par):
                b, nxt, prev = it.own, it.own + 1, it.own - 1
                if it.here:
                    move_maxima(b, 1, par)
                if it.after:
                    save_parts(k_parts, (k1_ready, k2_ready, k3_ready), k_saved, scratch["k"], PARTS, nxt)
                    save_parts(q_parts, (q1_ready, q2_ready, q3_ready), q_saved, scratch["q"], QSLOTS, nxt)
                    if it.before:
                        sp.wait_ge(t_filled, UNITS * b)
                        settle(sp)
                    sp.wait_ge(k_saved, 16 * PARTS * (nxt + 1))
                    settle(sp)
                    sp.wait_ge(q_saved, 16 * QSLOTS * (nxt + 1))
                    settle(sp)
                    for j in range(NG):
                        n = HG * T
                        sp.dma_start(k_stack[1 - par][0:STACK, HG * j:HG * (j + 1), :],
                                     window(scratch["k"], n * j, [[0, PARTS], [H * T, PARTS * HD], [1, n]])
                                     ).then_inc(stack_in[j], 16)
                        sp.dma_start(q_stack[1 - par][0:STACK, HG * j:HG * (j + 1), :],
                                     window(scratch["q"], n * j, [[HD * H * T, PARTS], [H * T, PARTS * HD], [1, n]])
                                     ).then_inc(stack_in[j], 16)
                if it.here:
                    move_maxima(b, 2, par)
                    move_maxima(b, 3, par)
                if it.before:
                    sp.wait_ge(probT_ready, prev + 1)
                    sp.dma_start(scratch["probs"].ap()[prev], probT[:]).then_inc(probT_out, 16)
                if it.after:
                    move_maxima(nxt, 0, 1 - par)

            sp.wait_ge(grow_ready, 7)
            sp.dma_start(scratch["gates"].ap().rearrange("k b d -> b k d"), grow[:]).then_inc(grow_out, 16)
            sp.wait_ge(grow_out, 16)
            sp.dma_start(gates[:], window(scratch["gates"], 0, [[0, P], [1, 2 * B * D]])).then_inc(gates_in, 16)
            pipeline(sp, iteration)
            sp.wait_ge(probT_out, 16 * B)

        @block.gpsimd
        def _(pool):
            nc.gpsimd.memset(ones[:], 1.0).then_inc(consts, 1)
            nc.gpsimd.memset(half[:], -0.5).then_inc(consts, 1)
            for i in range(2):
                nc.gpsimd.memset(v_ext[i][:], 0.0).then_inc(consts, 1)
                pool.wait_ge(consts, 3 + 2 * i)
                nc.gpsimd.memset(v_ext[i][:, :, :, HD:HD + 1], 1.0).then_inc(consts, 1)

            def split(rest, rest_ready, parts, second, third, saved, slots, bb):
                pool.wait_ge(rest_ready, bb + 1)
                pool.wait_ge(saved, 16 * slots * bb)
                settle(pool)
                nc.gpsimd.tensor_copy(parts[:, 1, :], rest[:]).then_inc(second, 1)
                pool.wait_ge(second, bb + 1)
                nc.gpsimd.tensor_tensor(parts[:, 2, :], rest[:], parts[:, 1, :], ALU.subtract).then_inc(third, 1)

            def maxima(bb, j):
                done = 3 * (NG * bb + j)
                pool.wait_ge(max_done, UNITS * bb + HG * NT * (j + 1))
                pool.wait_ge(m_filled[j], bb)
                parts = m_parts[:, j, :].rearrange("p (c n) -> p c n", c=PARTS)
                settle(pool)
                nc.gpsimd.tensor_copy(parts[:, 0, :], nmax[:, j, :]).then_inc(m_step, 1)
                pool.wait_ge(m_step, done + 1)
                nc.gpsimd.tensor_tensor(m_rest[:], nmax[:, j, :], parts[:, 0, :], ALU.subtract).then_inc(m_step, 1)
                pool.wait_ge(m_step, done + 2)
                settle(pool)
                nc.gpsimd.tensor_copy(parts[:, 1, :], m_rest[:]).then_inc(m_step, 1)
                pool.wait_ge(m_step, done + 3)
                nc.gpsimd.tensor_tensor(parts[:, 2, :], m_rest[:], parts[:, 1, :], ALU.subtract
                                        ).then_inc(m_parts_ready[j], 1)

            def iteration(it, par):
                b, nxt, prev = it.own, it.own + 1, it.own - 1
                if it.after:
                    pool.wait_ge(mv1_done, nxt + 1)
                    pool.wait_ge(hT_filled, nxt)
                    norm(nc, half, x_all[:, nxt], mv1, rstd1, r1_step, nxt, xh1, xh1_ready)
                if it.here:
                    maxima(b, 1)
                if it.after:
                    split(k_rest, k_rest_ready, k_parts, k2_ready, k3_ready, k_saved, PARTS, nxt)
                    split(q_rest, q_rest_ready, q_parts, q2_ready, q3_ready, q_saved, QSLOTS, nxt)
                if it.before:
                    pool.wait_ge(gates_in, 16)
                    pool.wait_ge(rest_in, 48)
                    pool.wait_ge(o_filled, prev)
                    nc.gpsimd.tensor_tensor(wo_gated[:], wo[:], gates[:, 0, prev, :], ALU.mult).then_inc(wog_ready, 1)
                    for t in range(NT):
                        last = nc.gpsimd.tensor_tensor(x_all[:, prev, t, :], x_all[:, prev, t, :],
                                                       gates[:, 1, prev, :], ALU.add)
                    last.then_inc(xbias_ready, 1)
                if it.here:
                    maxima(b, 2)
                if it.before:
                    pool.wait_ge(mv2_done, prev + 1)
                    pool.wait_ge(h2T_filled, prev)
                    norm(nc, half, x_all[:, prev], mv2, rstd2, r2_step, prev, xh2, xh2_ready)
                if it.here:
                    maxima(b, 3)
                if it.before:
                    pool.wait_ge(prob_ready, prev + 1)
                    settle(pool)
                    nc.gpsimd.tensor_copy(probs_tok[:, prev], prob_now[:]).then_inc(prob_kept, 1)
                if it.after:
                    maxima(nxt, 0)

            pipeline(pool, iteration)

        @block.scalar
        def _(act):
            act.wait_ge(c_in, 48)
            nc.scalar.activation(sig[:], cT[:], ACT.Exp, scale=-1.0).then_inc(sig_e, 1)

            def exponential(b, u):
                act.wait_ge(t_filled, UNITS * b + u + 1)
                if u % HG == 0 and not (isinstance(b, int) and b == 0 and u < 8):
                    act.wait_ge(av_done, H * b + u // HG - 1)
                nc.scalar.activation(probs[:, u % 8, :], ps_t[u % 3][:], ACT.Exp, scale=HD ** -0.5
                                     ).then_inc(exp_done, 1)

            def save_av(b, j):
                act.wait_ge(av_done, H * b + NT * (j + 1))
                if j >= 2:
                    act.wait_ge(avT_filled[j - 2], b + 1)
                else:
                    act.wait_ge(avT_filled[j + 2], b)
                nc.scalar.copy(att[:, j % 2, :], ps_av[:]).then_inc(av_saved, 1)

            def save_maxima(bb, j, bank):
                act.wait_ge(m_filled[j], bb + 1)
                act.wait_ge(m_in[j], 16 * bb)
                n = PARTS * HG * NT
                nc.scalar.copy(m_rows[:, j, :], as_bf16(bank)[0:n, 0:P]).then_inc(m_rows_ready[j], 1)

            def iteration(it, par):
                b, nxt, prev = it.own, it.own + 1, it.own - 1

                def shift_h():
                    act.wait_ge(hT_filled, nxt + 1)
                    act.wait_ge(v_filled, nxt)
                    act.wait_ge(mod_ready, 3)
                    nc.scalar.activation(hT[:], bank_a[:], ACT.Identity, scale=scale1[:, 0, 0, bass.ds(nxt, 1)],
                                         bias=mod[:, 0, SHIFT_A, bass.ds(nxt, 1)]).then_inc(hT_ready, 1)

                def first_part(which):
                    filled, saved, slots, parts, bank, bias, ready = {
                        "q": (q_filled, q_saved, QSLOTS, q_parts, bank_a, bq, q1_ready),
                        "k": (k_filled, k_saved, PARTS, k_parts, bank_b, bk, k1_ready)}[which]
                    act.wait_ge(filled, nxt + 1)
                    act.wait_ge(saved, 16 * slots * nxt)
                    act.wait_ge(wqkv_in, 96)
                    nc.scalar.activation(parts[:, 0, :], bank[:], ACT.Identity, bias=bias[:]).then_inc(ready, 1)

                def save_attT():
                    act.wait_ge(attT_filled, prev + 1)
                    act.wait_ge(o_filled, prev)
                    nc.scalar.copy(attT[:], bank_b[:]).then_inc(attT_ready, 1)

                def shift_h2():
                    act.wait_ge(h2T_filled, prev + 1)
                    act.wait_ge(lg_filled, prev)
                    nc.scalar.activation(h2T[:], bank_b[:], ACT.Identity, scale=scale1[:, 0, 1, bass.ds(prev, 1)],
                                         bias=mod[:, 0, SHIFT_B, bass.ds(prev, 1)]).then_inc(h2T_ready, 1)

                def exp_logits():
                    act.wait_ge(lg_ready, prev + 1)
                    act.wait_ge(prob_ready, prev)
                    nc.scalar.activation(lg_exp[:], lg[:], ACT.Exp).then_inc(lg_exp_ready, 1)

                def save_probT():
                    act.wait_ge(pT_filled, prev + 1)
                    act.wait_ge(probT_out, 16 * prev)
                    nc.scalar.copy(probT[:], bank_b[0:E, :]).then_inc(probT_ready, 1)

                work = {}
                if it.before:
                    work |= {5: lambda: save_av(prev, 3), 17: save_attT, 31: shift_h2, 37: exp_logits, 46: save_probT}
                if it.here:
                    work |= {6: lambda: save_maxima(b, 1, bank_b), 22: lambda: save_maxima(b, 2, bank_b),
                             38: lambda: save_maxima(b, 3, bank_b), 21: lambda: save_av(b, 0),
                             36: lambda: save_av(b, 1), 53: lambda: save_av(b, 2)}
                if it.after:
                    work |= {7: shift_h, 11: lambda: first_part("k"), 12: lambda: first_part("q"),
                             55: lambda: save_maxima(nxt, 0, bank_a)}
                for u in range(UNITS):
                    if it.here:
                        exponential(b, u)
                    if u in work:
                        work[u]()

            pipeline(act, iteration)

        @block.vector
        def _(dve):
            dve.wait_ge(sig_e, 1)
            nc.vector.tensor_scalar(sig[:], sig[:], 1.0, None, ALU.add).then_inc(silu, 1)
            dve.wait_ge(silu, 1)
            nc.vector.reciprocal(sig[:], sig[:]).then_inc(silu, 1)
            dve.wait_ge(silu, 2)
            nc.vector.tensor_tensor(siluT[:], cT[:], sig[:], ALU.mult).then_inc(silu, 1)
            nc.vector.tensor_copy(ident_b[:], ident[:]).then_inc(identb_ready, 1)

            def statistics(xin, st, mv, st_done, mv_done, bb):
                settle(dve)
                for t in range(NT):
                    last = nc.vector.bn_stats(st[:, t, :], xin[:, t, :])
                last.then_inc(st_done, 1)
                dve.wait_ge(st_done, bb + 1)
                settle(dve)
                for t in range(NT):
                    last = nc.vector.bn_aggr(mv[:, t, :], st[:, t, :])
                last.then_inc(mv_done, 1)

            def maximum(bs, js, v, u):
                dve.wait_ge(s_filled, UNITS * bs + HG * NT * js + v + 1)
                if v == 0:
                    dve.wait_ge(m_parts_ready[js], bs)
                n = (v % HG) * NT + v // HG
                nc.vector.tensor_reduce(nmax[:, js, n:n + 1], ps_s[u % 2][:], AX.X, ALU.max, negate=True
                                        ).then_inc(max_done, 1)

            def mod_vectors():
                dve.wait_ge(mod_mm, 1)
                v = bank_b[:, 0:12 * B].rearrange("p (l c b) -> p l c b", l=2, c=6)
                nc.vector.tensor_copy(mod[:], v).then_inc(mod_ready, 1)
                nc.vector.tensor_scalar(scale1[:, :, 0, :], v[:, :, SCALE_A, :], 1.0, None, ALU.add
                                        ).then_inc(mod_ready, 1)
                nc.vector.tensor_scalar(scale1[:, :, 1, :], v[:, :, SCALE_B, :], 1.0, None, ALU.add
                                        ).then_inc(mod_ready, 1)

            def gate_rows():
                dve.wait_ge(gate_mm, 1)
                v = bank_b[0:B, :].rearrange("p (k d) -> p k d", k=4)
                nc.vector.tensor_copy(graw[:], v).then_inc(gate_step, 1)
                nc.vector.tensor_scalar(gstep[:], v, 0.0, 2.0, ALU.is_ge, ALU.mult).then_inc(gate_step, 1)
                dve.wait_ge(gate_step, 2)
                nc.vector.scalar_tensor_tensor(gabs[:], graw[:], -1.0, graw[:], ALU.mult, ALU.max).then_inc(gate_step, 1)
                nc.vector.tensor_scalar(gsign[:], gstep[:], -1.0, None, ALU.add).then_inc(gate_step, 1)
                dve.wait_ge(gate_step, 4)
                nc.vector.scalar_tensor_tensor(gclamp[:], gabs[:], 0.25, gsign[:], ALU.max, ALU.mult
                                               ).then_inc(gate_step, 1)
                dve.wait_ge(gate_step, 5)
                dve.wait_ge(rest_in, 48)
                for to, of, by in ((0, 0, None), (1, 0, 0), (2, 1, None), (3, 2, None), (4, 2, 1), (5, 3, 2), (6, 3, 3)):
                    if by is None:
                        nc.vector.tensor_copy(grow[:, to, :], gclamp[:, of, :]).then_inc(grow_ready, 1)
                    else:
                        nc.vector.tensor_tensor(grow[:, to, :], gclamp[:, of, :], vectors[:, by, :], ALU.mult
                                                ).then_inc(grow_ready, 1)

            def iteration(it, par):
                b, nxt, prev = it.own, it.own + 1, it.own - 1

                def rest(which):
                    bank, bias, parts, rst, first, ready, third = {
                        "q": (bank_a, bq, q_parts, q_rest, q1_ready, q_rest_ready, q3_ready),
                        "k": (bank_b, bk, k_parts, k_rest, k1_ready, k_rest_ready, k3_ready)}[which]
                    dve.wait_ge(first, nxt + 1)
                    dve.wait_ge(third, nxt)
                    nc.vector.scalar_tensor_tensor(rst[:], bank[:], bias[:], parts[:, 0, :], ALU.add, ALU.subtract
                                                   ).then_inc(ready, 1)

                def values():
                    dve.wait_ge(v_filled, nxt + 1)
                    if it.before:
                        dve.wait_ge(av_done, H * b)
                    dve.wait_ge(consts, 6)
                    heads = bv[:].rearrange("p (h e) -> p h e", h=H).unsqueeze(1).to_broadcast([P, NT, H, HD])
                    nc.vector.tensor_tensor(v_ext[1 - par][:, :, :, 0:HD],
                                            bank_a[:].rearrange("p (t h e) -> p t h e", t=NT, h=H), heads,
                                            ALU.add).then_inc(v_ready, 1)

                def normalise(bb, j, bank):
                    dve.wait_ge(avT_filled[j], bb + 1)
                    v = bank[:].rearrange("p (t g n) -> p t g n", t=NT, g=HG)
                    dve.wait_ge(avT_read[j], bb)
                    nc.vector.reciprocal(rec[:, j], v[:, :, :, HD]).then_inc(rec_done[j], 1)
                    dve.wait_ge(rec_done[j], bb + 1)
                    if j == 0:
                        dve.wait_ge(attT_filled, bb)
                    out = att_tok[:, :, HG * HD * j:HG * HD * (j + 1)].rearrange("p t (g e) -> p t g e", g=HG)
                    nc.vector.tensor_tensor(out, v[:, :, :, 0:HD], rec[:, j].unsqueeze(3).to_broadcast([P, NT, HG, HD]),
                                            ALU.mult).then_inc(avT_read[j], 1)

                def residual():
                    dve.wait_ge(o_filled, prev + 1)
                    dve.wait_ge(xbias_ready, prev + 1)
                    nc.vector.tensor_tensor(x_all[:, prev], tokens(bank_a[:]), x_all[:, prev], ALU.add
                                            ).then_inc(x_ready, 1)
                    dve.wait_ge(x_ready, prev + 1)
                    dve.wait_ge(xh2_ready, prev)
                    statistics(x_all[:, prev], st2, mv2, st2_done, mv2_done, prev)

                def logits():
                    dve.wait_ge(lg_filled, prev + 1)
                    v = bank_a[:, 0:NT * E].rearrange("p (t e) -> p t e", t=NT)
                    nc.vector.tensor_reduce(lg_max[:], v, AX.X, ALU.max).then_inc(lg_step, 1)
                    dve.wait_ge(lg_step, 2 * prev + 1)
                    dve.wait_ge(lg_exp_ready, prev)
                    nc.vector.tensor_tensor(lg[:], v, lg_max[:].unsqueeze(2).to_broadcast([P, NT, E]), ALU.subtract
                                            ).then_inc(lg_ready, 1)

                def router():
                    dve.wait_ge(lg_exp_ready, prev + 1)
                    nc.vector.tensor_reduce(lg_sum[:], lg_exp[:], AX.X, ALU.add).then_inc(lg_step, 1)
                    dve.wait_ge(lg_step, 2 * prev + 2)
                    nc.vector.reciprocal(lg_inv[:], lg_sum[:]).then_inc(prob_inv, 1)
                    dve.wait_ge(prob_inv, prev + 1)
                    dve.wait_ge(pT_filled, prev)
                    dve.wait_ge(prob_kept, prev)
                    nc.vector.tensor_tensor(prob_now[:], lg_exp[:], lg_inv[:].unsqueeze(2).to_broadcast([P, NT, E]),
                                            ALU.mult).then_inc(prob_ready, 1)

                if it.after:
                    if not it.here:
                        dve.wait_ge(x0_in, 16)
                    elif not it.before:
                        dve.wait_ge(x_in, 16)
                    dve.wait_ge(xh1_ready, nxt)
                    statistics(x_all[:, nxt], st1, mv1, st1_done, mv1_done, nxt)
                work = {}
                if it.after and not it.here:
                    work |= {0: mod_vectors, 18: gate_rows}
                if it.before:
                    work |= {9: lambda: normalise(prev, 3, bank_b), 22: residual, 35: logits, 40: router}
                if it.here:
                    work |= {26: lambda: normalise(b, 0, bank_a), 43: lambda: normalise(b, 1, bank_a),
                             59: lambda: normalise(b, 2, bank_b)}
                if it.after:
                    work |= {11: lambda: rest("k"), 13: lambda: rest("q"), 16: values}
                for u in range(UNITS):
                    bs, js, there = scores_of(u, it)
                    if there:
                        maximum(bs, js, u % (HG * NT), u)
                    if u in work:
                        work[u]()

            pipeline(dve, iteration)

        @block.tensor
        def _(pe):
            def quarter(t):
                return slice(P * t, P * (t + 1))

            pe.wait_ge(c_in, 48)
            pe.wait_ge(silu, 3)
            for l in range(2):
                for c in range(6):
                    n = (6 * l + c) * B
                    last = nc.tensor.matmul(bank_b[:, n:n + B], wmod[:, l, c * D:(c + 1) * D], siluT[:, l, :],
                                            start=True, stop=True)
            last.then_inc(mod_mm, 1)

            def score(bs, js, v, u, par):
                if v == 0:
                    pe.wait_ge(stack_in[js], 32 * (bs + 1))
                done = UNITS * bs + HG * NT * js + v
                if not (isinstance(done, int) and done < 2):
                    pe.wait_ge(max_done, done - 1)
                h, t = HG * js + v % HG, v // HG
                nc.tensor.matmul(ps_s[u % 2][:], q_stack[par][0:STACK, h, quarter(t)], k_stack[par][0:STACK, h, :],
                                 start=True, stop=True).then_inc(s_filled, 1)

            def score_t(b, u, par):
                j, t, g = u // (HG * NT), u // HG % NT, u % HG
                if u % (HG * NT) == 0:
                    pe.wait_ge(m_in[j], 16 * (b + 1))
                    pe.wait_ge(ones_in, 32)
                if u >= 3:
                    pe.wait_ge(exp_done, UNITS * b + u - 2)
                elif not (isinstance(b, int) and b == 0):
                    last = max(w for w in range(UNITS) if w % 3 == u)
                    pe.wait_ge(exp_done, UNITS * b - UNITS + last + 1)
                h = HG * j + g
                nc.tensor.matmul(ps_t[u % 3][:], k_stack[par][0:STACK + PARTS, h, quarter(t)],
                                 q_stack[par][0:STACK + PARTS, h, :], start=True, stop=True).then_inc(t_filled, 1)

            def weigh(b, k, par):
                j, t = k // NT, k % NT
                pe.wait_ge(exp_done, UNITS * b + HG * (k + 1))
                pe.wait_ge(v_ready, b + 1)
                if t == 0:
                    pe.wait_ge(av_saved, NG * b + j)
                for g in range(HG):
                    last = nc.tensor.matmul(ps_av[32 * g:32 * (g + 1), :], v_ext[par][:, t, HG * j + g, :],
                                            probs[:, (HG * k + g) % 8, :], start=(t == 0), stop=(t == NT - 1))
                last.then_inc(av_done, 1)

            def transposes(bank, of, filled):
                for t in range(NT):
                    last = nc.tensor.transpose(bank[:, quarter(t)], of(t), ident[:])
                last.then_inc(filled, 1)

            def iteration(it, par):
                b, nxt, prev = it.own, it.own + 1, it.own - 1

                def free(*choices):
                    for there, s, n in choices:
                        if there:
                            pe.wait_ge(s, n)
                            return

                def norm_T():
                    pe.wait_ge(xh1_ready, nxt + 1)
                    free((it.here, m_rows_ready[0], b + 1))
                    transposes(bank_a, lambda t: xh1[:, t, :], hT_filled)

                def project_k():
                    pe.wait_ge(hT_ready, nxt + 1)
                    pe.wait_ge(wqkv_in, 96)
                    free((it.before, avT_read[3], prev + 1), (it.here, m_rows_ready[1], b + 1), (True, mod_ready, 3))
                    nc.tensor.matmul(bank_b[:], wk[:], hT[:], start=True, stop=True).then_inc(k_filled, 1)

                def project_q():
                    pe.wait_ge(hT_ready, nxt + 1)
                    nc.tensor.matmul(bank_a[:], wq[:], hT[:], start=True, stop=True).then_inc(q_filled, 1)

                def project_v():
                    free((True, q_rest_ready, nxt + 1))
                    for t in range(NT):
                        last = nc.tensor.matmul(bank_a[:, quarter(t)], hT[:, quarter(t)], wv[:], start=True, stop=True)
                    last.then_inc(v_filled, 1)

                def gate_products():
                    free((True, k_rest_ready, nxt + 1))
                    for k, (l, c) in enumerate(((0, GATE_A), (0, GATE_B), (1, GATE_A), (1, GATE_B))):
                        last = nc.tensor.matmul(bank_b[0:B, k * D:(k + 1) * D], siluT[:, l, :],
                                                wmod[:, l, c * D:(c + 1) * D], start=True, stop=True)
                    last.then_inc(gate_mm, 1)

                def heads_T(bb, j, bank, *choices):
                    free(*choices)
                    pe.wait_ge(av_saved, NG * bb + j + 1)
                    transposes(bank, lambda t: att[:, j % 2, quarter(t)], avT_filled[j])

                def maxima_T(bb, j, bank, *choices):
                    free(*choices)
                    pe.wait_ge(m_parts_ready[j], bb + 1)
                    pe.wait_ge(identb_ready, 1)
                    settle(pe)
                    n = PARTS * HG * NT
                    nc.tensor.transpose(as_bf16(bank)[0:n, 0:P], m_parts[:, j, :], ident_b[:]).then_inc(m_filled[j], 1)

                def tokens_T():
                    pe.wait_ge(avT_read[3], prev + 1)
                    free((it.after, k_rest_ready, nxt + 1))
                    transposes(bank_b, lambda t: att_tok[:, t, :], attT_filled)

                def project_o():
                    pe.wait_ge(attT_ready, prev + 1)
                    pe.wait_ge(wog_ready, prev + 1)
                    free((it.after, v_ready, nxt + 1), (it.here, m_rows_ready[0], b + 1), (True, avT_read[1], prev + 1))
                    for t in range(NT):
                        last = nc.tensor.matmul(bank_a[:, quarter(t)], attT[:, quarter(t)], wo_gated[:],
                                                start=True, stop=True)
                    last.then_inc(o_filled, 1)

                def norm2_T():
                    pe.wait_ge(xh2_ready, prev + 1)
                    free((it.here, m_rows_ready[2], b + 1), (True, attT_ready, prev + 1))
                    transposes(bank_b, lambda t: xh2[:, t, :], h2T_filled)

                def logits():
                    pe.wait_ge(h2T_ready, prev + 1)
                    free((it.here, avT_read[0], b + 1), (True, x_ready, prev + 1))
                    for t in range(NT):
                        last = nc.tensor.matmul(bank_a[:, E * t:E * (t + 1)], h2T[:, quarter(t)], gate_w[:],
                                                start=True, stop=True)
                    last.then_inc(lg_filled, 1)

                def probs_T():
                    pe.wait_ge(prob_ready, prev + 1)
                    free((it.here, m_rows_ready[3], b + 1), (True, h2T_ready, prev + 1))
                    for t in range(NT):
                        last = nc.tensor.transpose(bank_b[0:E, quarter(t)], prob_now[:, t, :], ident[:])
                    last.then_inc(pT_filled, 1)

                work = {}
                if it.after and not it.here:
                    work |= {16: gate_products}
                if it.before:
                    work |= {8: lambda: heads_T(prev, 3, bank_b, (it.here, m_rows_ready[1], b + 1),
                                                (True, avT_read[2], prev + 1)),
                             17: tokens_T, 20: project_o, 30: norm2_T, 34: logits, 45: probs_T}
                if it.here:
                    work |= {4: lambda: maxima_T(b, 1, bank_b, (it.before, avT_read[2], b), (True, gate_step, 2)),
                             21: lambda: maxima_T(b, 2, bank_b, (it.before, attT_ready, prev + 1),
                                                  (True, k_rest_ready, nxt + 1)),
                             25: lambda: heads_T(b, 0, bank_a, (it.before, x_ready, prev + 1), (True, v_ready, nxt + 1)),
                             37: lambda: maxima_T(b, 3, bank_b, (it.before, h2T_ready, prev + 1),
                                                  (True, m_rows_ready[2], b + 1)),
                             41: lambda: heads_T(b, 1, bank_a, (it.before, lg_ready, prev + 1),
                                                 (True, avT_read[0], b + 1)),
                             57: lambda: heads_T(b, 2, bank_b, (it.before, probT_ready, prev + 1),
                                                 (True, m_rows_ready[3], b + 1))}
                if it.after:
                    work |= {6: norm_T, 10: project_k, 11: project_q, 14: project_v,
                             53: lambda: maxima_T(nxt, 0, bank_a, (it.here, avT_read[1], b + 1),
                                                  (True, v_ready, nxt + 1))}
                for u in range(UNITS):
                    bs, js, there = scores_of(u, it)
                    if there:
                        score(bs, js, u % (HG * NT), u, par if js >= NG // 2 else 1 - par)
                    if it.here:
                        score_t(b, u, par)
                    if u == HG - 1 and it.before:
                        weigh(prev, H - 1, 1 - par)
                    elif u % HG == HG - 1 and u >= HG and it.here:
                        weigh(b, u // HG - 1, par)
                    if u in work:
                        work[u]()

            pipeline(pe, iteration)


class Stage(Batch):

    def __init__(self, own, before=True, here=True, after=True, later=True):
        super().__init__(own, before, here, after)
        self.later = later


def program_experts(nc, io, keep, scratch, held):
    ctx = ExitStack()
    with ctx:
        def sb(name, shape, dt=F32):
            return ctx.enter_context(nc.sbuf_tensor(name, shape, dt))

        def pb(name, shape, dt=F32):
            return ctx.enter_context(nc.psum_tensor(name, shape, dt))

        def sem(name):
            held.append(nc.alloc_semaphore(name=name))
            return held[-1]

        x_all, probs_tok, mod, scale1, ident = (
            keep["x"], keep["probs"], keep["mod"], keep["scale1"], keep["ident"])

        w1_0 = sb("w1_0", [P, E, F])
        w2_0 = sb("w2_0", [P, E, NF, D])
        w1_high = sb("w1_high", [P, E, F], F32R)
        w1_low = sb("w1_low", [P, E, F], F32R)
        w2_1 = sb("w2_1", [P, E, NF, D])
        b1 = sb("b1", [P, E, NF])
        b2 = sb("b2", [E, D])
        wq1 = sb("wq1", [P, P])
        bq1 = sb("bq1", [P, 1])
        wd = sb("wd", [P, R])
        bd = sb("bd", [R, 1])
        wu = sb("wu", [R + 1, 2 * D])
        wo1 = sb("wo1", [P, D])
        gate1 = sb("gate1", [P, E])
        shared_w = sb("shared_w", [P, D])
        shared_b = sb("shared_b", [P, D])
        slots = sb("slots", [P, KSEL])
        block_mask = sb("block_mask", [P, P + H])
        lower = sb("lower", [P, E, E])
        half = sb("half_b", [P, NT])
        acc = [sb(f"acc{i}", [P, NT, D]) for i in range(2)]
        xh_o = sb("xh_o", [P, NT, D])
        x_done = sb("x_done", [P, NT, D])
        rows = [acc[i][0:B * E].rearrange("p t d -> p (t d)") for i in range(2)]
        taken = xh_o[0:B * E].rearrange("p t d -> p (t d)")
        rank = x_done[0:B * E].rearrange("p t d -> p (t d)")
        best = sb("best", [B * E, 8])
        pos_tok = sb("pos_tok", [P, B, NT, E])
        st_a = sb("st_a", [P, NT, 6])
        mv_a = sb("mv_a", [P, NT, 2])
        rs_a = sb("rs_a", [P, 3, NT])
        xh_a = sb("xh_a", [P, NT, D])
        xha_high = sb("xha_high", [P, NT, D], F32R)
        xha_low = sb("xha_low", [P, NT, D], F32R)
        sel = sb("sel", [P, NT, E // 2, KSEL], F32R)
        xin = sb("xin", [P, E, KSEL])
        hid0 = [sb(f"hid0_{i}", [P, NF, KSEL]) for i in range(2)]
        gsel = [sb(f"gsel{i}", [P, NT, KSEL]) for i in range(2)]
        gselT = [sb(f"gselT{i}", [P, T]) for i in range(2)]
        y0 = [sb(f"y0_{i}", [P, D]) for i in range(2)]
        gated0 = sb("gated0", [P, NT, D])
        st_b = sb("st_b", [P, NT, 6])
        mv_b = sb("mv_b", [P, NT, 2])
        rs_b = sb("rs_b", [P, 3, NT])
        xh_b = sb("xh_b", [P, NT, D])
        hT1 = sb("hT1", [P, T])
        latent = sb("latent", [R + 1, T])
        q_pos = sb("q_pos", [P, T])
        q_exp = sb("q_exp", [P, T])
        k_exp = sb("k_exp", [P, T])
        k_phi = sb("k_phi", [P, NT, D])
        v1 = sb("v1", [P, NT, D + 1])
        context = sb("context", [P, P + H])
        den = sb("den", [P, NT * H])
        den_inv = sb("den_inv", [P, NT * H])
        att1 = sb("att1", [P, NT, D])
        attT1 = sb("attT1", [P, T])
        wo1_gated = sb("wo1_gated", [P, D])
        st_f = sb("st_f", [P, NT, 6])
        mv_f = sb("mv_f", [P, NT, 2])
        rs_f = sb("rs_f", [P, 3, NT])
        xh_f = sb("xh_f", [P, NT, D])
        hT_f = sb("hT_f", [P, T])
        hTf_high = [sb(f"hTf_high{i}", [P, T], F32R) for i in range(2)]
        hTf_low = [sb(f"hTf_low{i}", [P, T], F32R) for i in range(2)]
        lmax = sb("lmax", [P, NT])
        lshift = sb("lshift", [P, NT, E])
        lexp = sb("lexp", [P, NT, E])
        lsum = sb("lsum", [P, NT])
        linv = sb("linv", [P, NT])
        prob = sb("prob", [P, NT, E])
        above = sb("above", [P, NT, E, E])
        tied = sb("tied", [P, NT, E, E])
        ahead = sb("ahead", [P, NT, E])
        top2 = sb("top2", [P, NT, E])
        tsum = sb("tsum", [P, NT])
        tinv = sb("tinv", [P, NT])
        comb = [sb(f"comb{i}", [P, NT, E]) for i in range(2)]
        combT = sb("combT", [E, T])
        sh = sb("sh", [P, NT, D])
        hid1 = [sb(f"hid1_{i}", [P, NF, T]) for i in range(2)]
        gate0 = sb("gate0", [P, D])
        gate_att1 = sb("gate_att1", [P, 2, D])
        gate_end = sb("gate_end", [P, 2, D])
        st_o = sb("st_o", [P, NT, 6])
        mv_o = sb("mv_o", [P, NT, 2])
        rs_o = sb("rs_o", [P, 3, NT])

        ps_z = [pb(f"ps_z{i}", [P, T]) for i in range(2)]
        ps_o = pb("ps_o", [P, T])
        a0 = pb("a0", [P, T])
        a1 = pb("a1", [P, T])
        a2 = pb("a2", [P, T])
        b0_ = pb("b0_", [P, T])
        b1_ = pb("b1_", [P, T])

        probs_in, small_in, w0_in, w1_in, w2_in, consts = (
            sem(n) for n in "probs_in small_in w0_in w1_in w2_in consts_b".split())
        w1_step, w1_ready, gate0_in, gate_att1_in, gate_end_in = (
            sem(n) for n in "w1_step w1_ready gate0_in gate_att1_in gate_end_in".split())
        xha_rounded, xha_split, hTf_rounded, hTf_split = (
            sem(n) for n in "xha_rounded xha_split hTf_rounded hTf_split".split())
        best_found, best_taken, rank_step, rank_ready, pos_filled, pos_ready = (
            sem(n) for n in "best_found best_taken rank_step rank_ready pos_filled pos_ready".split())
        sta_done, mva_done, ra_step, xha_ready, sel_ready = (
            sem(n) for n in "sta_done mva_done ra_step xha_ready sel_ready".split())
        g_filled, xin_ready, z0_filled, hid0_ready, gsel_ready, t_filled, gselT_ready, y0_filled, y0_ready = (
            sem(n) for n in "g_filled xin_ready z0_filled hid0_ready gsel_ready tb_filled gselT_ready "
            "y0_filled y0_ready".split())
        sc_filled, gated0_ready, x0_ready = (sem(n) for n in "sc_filled gated0_ready x0_ready".split())
        stb_done, mvb_done, rb_step, xhb_ready, hT1_filled, hT1_ready = (
            sem(n) for n in "stb_done mvb_done rb_step xhb_ready hT1_filled hT1_ready".split())
        lat_filled, lat_ready, q1_filled, qpos_ready, qmin_ready, qexp_ready, qphi_ready = (
            sem(n) for n in "lat_filled lat_ready qb_filled qpos_ready qmin_ready qexp_ready qphi_ready".split())
        uk_filled, kmin_ready, kexp_ready, kphi_ready, uv_filled, v1_ready = (
            sem(n) for n in "uk_filled kmin_ready kexp_ready kphi_ready uv_filled v1_ready".split())
        ctx_filled, ctx_ready, num_filled, den_step, den_ready, att1_ready, attT1_filled, attT1_ready = (
            sem(n) for n in "ctx_filled ctx_ready num_filled den_step den_ready att1_ready attT1_filled "
            "attT1_ready".split())
        wo1g_ready, xb1_ready, o1_filled, x1_ready = (sem(n) for n in "wo1g_ready xb1_ready o1_filled x1_ready".split())
        stf_done, mvf_done, rf_step, xhf_ready, hTf_filled, hTf_ready = (
            sem(n) for n in "stf_done mvf_done rf_step xhf_ready hTf_filled hTf_ready".split())
        l_sum, l_inv = sem("l_sum"), sem("l_inv")
        l_filled, l_step, lshift_ready, lexp_ready, top_step, comb_ready, combT_filled, combT_ready = (
            sem(n) for n in "l_filled l_step lshift_ready lexp_ready top_step comb_ready combT_filled "
            "combT_ready".split())
        sh_filled, sh_ready, shg_ready, b2_filled, acc_ready = (
            sem(n) for n in "sh_filled sh_ready shg_ready b2_filled acc_ready".split())
        z_filled, hid1_ready, o_filled, o_added = (sem(n) for n in "z_filled hid1_ready ob_filled o_added".split())
        sto_done, mvo_done, ro_step, xho_ready, outg_ready, xb2_ready, out_ready, stored = (
            sem(n) for n in "sto_done mvo_done ro_step xho_ready outg_ready xb2_ready out_ready stored".split())

        Q = 4 * E
        block = ctx.enter_context(nc.Block())

        def pipeline(eng, iteration):
            iteration(Stage(-2, False, False, False), 0)
            iteration(Stage(-1, False, False), 1)
            iteration(Stage(0, False), 0)
            iteration(Stage(1), 1)
            with eng.Fori(0, (B - 4) // 2) as i:
                iteration(Stage(2 * i + 2), 0)
                iteration(Stage(2 * i + 3), 1)
            iteration(Stage(B - 2, later=False), B % 2)
            iteration(Stage(B - 1, after=False, later=False), (B - 1) % 2)
            iteration(Stage(B, here=False, after=False, later=False), B % 2)

        def tokens(ap):
            return ap.rearrange("p (t n) -> p t n", t=NT)

        def quarter(t):
            return slice(P * t, P * (t + 1))

        def over_tokens(ap):
            return ap.unsqueeze(1).to_broadcast([P, NT, D])

        @block.sync
        def _(sp):
            sp.dma_start(rows[0], scratch["probs"].ap().rearrange("b e t -> (b e) t")).then_inc(probs_in, 16)
            for tile, name in ((slots, "slots"), (shared_b, "shared_b")):
                sp.dma_start(tile[:], io[name].partition_broadcast(P)).then_inc(small_in, 16)
            sp.dma_start(lower[:], io["lower"].partition_broadcast(P)).then_inc(small_in, 16)
            for tile, name in ((block_mask, "block_mask"), (b1, "b1"), (b2, "b2"), (wq1, "wq1"), (bq1, "bq1"),
                               (wd, "wd"), (bd, "bd"), (wu, "wu"), (wo1, "wo1"), (gate1, "gate1"),
                               (shared_w, "shared_w")):
                sp.dma_start(tile[:], io[name]).then_inc(small_in, 16)
            sp.dma_start(w1_0[:], io["w1_0"].rearrange("e d f -> d e f")).then_inc(w0_in, 16)
            sp.dma_start(w2_0[:], io["w2_0"].rearrange("e (n p) d -> p e n d", p=P)).then_inc(w0_in, 16)
            for i in range(2):
                sp.dma_start(hid1[i][:], io["w1_1"][E // 2 * i:E // 2 * (i + 1)].rearrange("e d f -> d e f")
                             ).then_inc(w1_in, 16)
            sp.dma_start(w2_1[:], io["w2_1"].rearrange("e (n p) d -> p e n d", p=P)).then_inc(w2_in, 16)

            def gate_rows(tile, k, n, bb, loaded):
                sp.dma_start(tile, scratch["gates"].ap()[k:k + n, bass.ds(bb, 1), :].partition_broadcast(P)
                             ).then_inc(loaded, 16)

            gate_rows(gate_att1[:], 3, 2, 0, gate_att1_in)

            def iteration(it, par):
                nxt, nn, prev = it.own + 1, it.own + 2, it.own - 1
                if it.before:
                    sp.wait_ge(xb2_ready, prev)
                    sp.wait_ge(outg_ready, prev)
                    settle(sp)
                    gate_rows(gate_end[:], 5, 2, prev, gate_end_in)
                if it.later:
                    sp.wait_ge(gated0_ready, nn)
                    settle(sp)
                    gate_rows(gate0[:], 2, 1, nn, gate0_in)
                if it.after and it.later:
                    sp.wait_ge(xb1_ready, nxt + 1)
                    sp.wait_ge(wo1g_ready, nxt + 1)
                    settle(sp)
                    gate_rows(gate_att1[:], 3, 2, nxt + 1, gate_att1_in)
                if it.before:
                    sp.wait_ge(out_ready, prev + 1)
                    sp.dma_start(io["out"][prev].rearrange("(t p) d -> p t d", p=P), x_done[:]).then_inc(stored, 16)

            pipeline(sp, iteration)
            sp.wait_ge(stored, 16 * B)

        @block.gpsimd
        def _(pool):
            nc.gpsimd.memset(half[:], -0.5).then_inc(consts, 1)
            pool.wait_ge(consts, 1)
            nc.gpsimd.memset(latent[R:R + 1, :], 1.0).then_inc(consts, 1)
            pool.wait_ge(consts, 2)
            nc.gpsimd.memset(v1[:, :, D:D + 1], 1.0).then_inc(consts, 1)
            pool.wait_ge(consts, 3)

            def add_vector(bb, row, ready):
                settle(pool)
                for t in range(NT):
                    last = nc.gpsimd.tensor_tensor(x_all[:, bb, t, :], x_all[:, bb, t, :], row, ALU.add)
                last.then_inc(ready, 1)

            def split_w1():
                pool.wait_ge(w1_in, 32)
                for i in range(2):
                    half_of = slice(E // 2 * i, E // 2 * (i + 1))
                    nc.gpsimd.tensor_copy(w1_high[:, half_of], hid1[i][:]).then_inc(w1_step, 1)
                    pool.wait_ge(w1_step, i + 1)
                    nc.gpsimd.tensor_tensor(w1_low[:, half_of], hid1[i][:], w1_high[:, half_of], ALU.subtract
                                            ).then_inc(w1_ready, 1)

            def iteration(it, par):
                b, nxt, nn, prev = it.own, it.own + 1, it.own + 2, it.own - 1
                if it.later:
                    pool.wait_ge(mva_done, nn + 1)
                    pool.wait_ge(xha_split, nn)
                    norm(nc, half, x_all[:, nn], mv_a, rs_a, ra_step, nn, xh_a, xha_ready)
                if it.after:
                    pool.wait_ge(mvb_done, nxt + 1)
                    pool.wait_ge(hT1_filled, nxt)
                    norm(nc, half, x_all[:, nxt], mv_b, rs_b, rb_step, nxt, xh_b, xhb_ready)
                elif it.later:
                    split_w1()
                if it.after:
                    pool.wait_ge(xhb_ready, nxt + 1)
                    pool.wait_ge(gate_att1_in, 16 * (nxt + 1))
                    add_vector(nxt, gate_att1[:, 1, :], xb1_ready)
                    pool.wait_ge(o1_filled, nxt)
                    pool.wait_ge(small_in, 224)
                    nc.gpsimd.tensor_tensor(wo1_gated[:], wo1[:], gate_att1[:, 0, :], ALU.mult).then_inc(wo1g_ready, 1)
                if it.before:
                    pool.wait_ge(gate_end_in, 16 * (prev + 1))
                    add_vector(prev, gate_end[:, 1, :], xb2_ready)
                    pool.wait_ge(mvo_done, prev + 1)
                    pool.wait_ge(out_ready, prev)
                    norm(nc, half, acc[1 - par][:], mv_o, rs_o, ro_step, prev, xh_o, xho_ready)
                if it.after:
                    pool.wait_ge(qexp_ready, nxt + 1)
                    pool.wait_ge(qpos_ready, nxt + 1)
                    nc.gpsimd.tensor_tensor(q_exp[:], q_exp[:], q_pos[:], ALU.add).then_inc(qphi_ready, 1)
                    pool.wait_ge(mvf_done, nxt + 1)
                    pool.wait_ge(hTf_filled, nxt)
                    norm(nc, half, x_all[:, nxt], mv_f, rs_f, rf_step, nxt, xh_f, xhf_ready)
                if it.later:
                    pool.wait_ge(gated0_ready, nn + 1)
                    settle(pool)
                    nc.gpsimd.tensor_tensor(x_all[:, nn], x_all[:, nn], gated0[:], ALU.add).then_inc(x0_ready, 1)

            pipeline(pool, iteration)

        @block.scalar
        def _(act):
            def gelu_quarter(b, q, par):
                e, n = q // 4, q % 4
                act.wait_ge(z_filled, Q * b + q + 1)
                if n == 0 and (e or not (isinstance(b, int) and b == 0)):
                    act.wait_ge(o_filled, E * b + e - 1)
                nc.scalar.activation(hid1[e % 2][:, n, :], ps_z[q % 2][:], ACT.Gelu, bias=b1[:, e, n:n + 1]
                                     ).then_inc(hid1_ready, 1)

            def iteration(it, par):
                b, nxt, nn, prev = it.own, it.own + 1, it.own + 2, it.own - 1

                def gathered(g):
                    act.wait_ge(g_filled, 2 * nn + g + 1)
                    act.wait_ge(z0_filled, E * nn)
                    settle(act)
                    nc.scalar.activation(xin[:, 4 * g:4 * g + 4, :].rearrange("p e k -> p (e k)"), (a0, a1)[g][:],
                                         ACT.Identity, scale=scale1[:, 0, 1, bass.ds(nn, 1)],
                                         bias=mod[:, 0, SHIFT_B, bass.ds(nn, 1)]).then_inc(xin_ready, 1)

                def gelu0(e):
                    act.wait_ge(z0_filled, E * nn + e + 1)
                    if e >= 2 or not (isinstance(nn, int) and nn == 0):
                        act.wait_ge(y0_filled, E * nn + e - 1)
                    nc.scalar.activation(hid0[e % 2][:].rearrange("p n k -> p (n k)"), a0[:], ACT.Gelu
                                         ).then_inc(hid0_ready, 1)

                def save_gselT(e):
                    act.wait_ge(t_filled, E * nn + e + 1)
                    if e >= 2 or not (isinstance(nn, int) and nn == 0):
                        act.wait_ge(sc_filled, E * nn + e - 1)
                    nc.scalar.copy(gselT[e % 2][:], a1[:]).then_inc(gselT_ready, 1)

                def shift_1():
                    act.wait_ge(hT1_filled, nxt + 1)
                    act.wait_ge(q1_filled, nxt)
                    nc.scalar.activation(hT1[:], b0_[:], ACT.Identity, scale=scale1[:, 1, 0, bass.ds(nxt, 1)],
                                         bias=mod[:, 1, SHIFT_A, bass.ds(nxt, 1)]).then_inc(hT1_ready, 1)

                def save_latent():
                    act.wait_ge(lat_filled, nxt + 1)
                    act.wait_ge(uv_filled, nxt)
                    act.wait_ge(small_in, 224)
                    nc.scalar.activation(latent[0:R, :], b1_[0:R, :], ACT.Identity, bias=bd[:]).then_inc(lat_ready, 1)

                def q_positive():
                    act.wait_ge(q1_filled, nxt + 1)
                    act.wait_ge(qphi_ready, nxt)
                    nc.scalar.activation(q_pos[:], b0_[:], ACT.Relu, bias=bq1[:]).then_inc(qpos_ready, 1)

                def exp_qk():
                    act.wait_ge(qmin_ready, nxt + 1)
                    nc.scalar.activation(q_exp[:], q_exp[:], ACT.Exp).then_inc(qexp_ready, 1)
                    act.wait_ge(kmin_ready, nxt + 1)
                    nc.scalar.activation(k_exp[:], k_exp[:], ACT.Exp).then_inc(kexp_ready, 1)

                def save_v1():
                    act.wait_ge(uv_filled, nxt + 1)
                    act.wait_ge(ctx_filled, nxt)
                    nc.scalar.copy(v1[:, :, 0:D], tokens(b0_[:])).then_inc(v1_ready, 1)

                def save_attT1():
                    act.wait_ge(attT1_filled, nxt + 1)
                    act.wait_ge(o1_filled, nxt)
                    nc.scalar.copy(attT1[:], b0_[:]).then_inc(attT1_ready, 1)

                def shift_f():
                    act.wait_ge(hTf_filled, nxt + 1)
                    act.wait_ge(sh_filled, nxt)
                    act.wait_ge(hTf_split, nxt)
                    nc.scalar.activation(hT_f[:], b0_[:], ACT.Identity, scale=scale1[:, 1, 1, bass.ds(nxt, 1)],
                                         bias=mod[:, 1, SHIFT_B, bass.ds(nxt, 1)]).then_inc(hTf_ready, 1)
                    act.wait_ge(hTf_ready, nxt + 1)
                    if it.before:
                        act.wait_ge(z_filled, Q * b)
                    nc.scalar.copy(hTf_high[1 - par][:], hT_f[:]).then_inc(hTf_rounded, 1)

                def exp_router():
                    act.wait_ge(lshift_ready, nxt + 1)
                    act.wait_ge(comb_ready, nxt)
                    nc.scalar.activation(lexp[:], lshift[:], ACT.Exp).then_inc(lexp_ready, 1)

                def gelu_shared():
                    act.wait_ge(sh_ready, nxt + 1)
                    nc.scalar.activation(sh[:], sh[:], ACT.Gelu).then_inc(shg_ready, 1)

                def save_combT():
                    act.wait_ge(combT_filled, nxt + 1)
                    act.wait_ge(b2_filled, nxt)
                    nc.scalar.copy(combT[:], b1_[0:E, :]).then_inc(combT_ready, 1)

                work = {q: [] for q in range(Q)}
                if it.after:
                    for q, f in ((4, shift_1), (6, save_latent), (8, q_positive), (10, exp_qk), (11, save_v1),
                                 (20, save_attT1), (25, shift_f), (27, exp_router), (29, gelu_shared),
                                 (30, save_combT)):
                        work[q].append(f)
                if it.later:
                    work[3].append(lambda: gathered(0))
                    work[5].append(lambda: gathered(1))
                    for e in range(E):
                        work[5 + 3 * e].append(lambda e=e: save_gselT(e))
                        work[6 + 3 * e].append(lambda e=e: gelu0(e))
                for q in range(Q):
                    if it.here:
                        gelu_quarter(b, q, par)
                    for f in work[q]:
                        f()

            pipeline(act, iteration)

        @block.vector
        def _(dve):
            dve.wait_ge(probs_in, 16)
            for r in range(KSEL // 8):
                if r:
                    dve.wait_ge(best_taken, r)
                nc.vector.max(best[:], rows[r % 2]).then_inc(best_found, 1)
                dve.wait_ge(best_found, r + 1)
                nc.vector.match_replace(out=rows[(r + 1) % 2], in_to_replace=best[:], in_values=rows[r % 2],
                                        imm_value=-1.0).then_inc(best_taken, 1)
            dve.wait_ge(best_taken, KSEL // 8)
            nc.vector.tensor_scalar(taken, rows[0], 0.0, None, ALU.is_lt).then_inc(rank_step, 1)
            dve.wait_ge(rank_step, 1)
            nc.vector.tensor_tensor_scan(rows[1], taken, taken, 0.0, ALU.add, ALU.max).then_inc(rank_step, 1)
            dve.wait_ge(rank_step, 2)
            nc.vector.tensor_tensor(rank, rows[1], taken, ALU.mult).then_inc(rank_ready, 1)
            dve.wait_ge(pos_filled, 1)
            nc.vector.tensor_copy(pos_tok[:], a0[:, 0:NT * B * E].rearrange("p (t b e) -> p b t e", t=NT, b=B)
                                  ).then_inc(pos_ready, 1)
            dve.wait_ge(pos_ready, 1)
            dve.wait_ge(small_in, 224)

            def statistics(xin_, st, mv, st_done, mv_done, bb, read):
                dve.wait_ge(read, bb)
                settle(dve)
                for t in range(NT):
                    last = nc.vector.bn_stats(st[:, t, :], xin_[:, t, :])
                last.then_inc(st_done, 1)
                dve.wait_ge(st_done, bb + 1)
                settle(dve)
                for t in range(NT):
                    last = nc.vector.bn_aggr(mv[:, t, :], st[:, t, :])
                last.then_inc(mv_done, 1)

            def iteration(it, par):
                b, nxt, nn, prev = it.own, it.own + 1, it.own + 2, it.own - 1

                def add_expert(bb, e, pp):
                    dve.wait_ge(o_filled, E * bb + e + 1)
                    if e == 0:
                        dve.wait_ge(acc_ready, bb + 1)
                    dve.wait_ge(o_added, E * bb + e)
                    for t in range(NT):
                        last = nc.vector.scalar_tensor_tensor(acc[pp][:, t, :], ps_o[:, quarter(t)],
                                                              comb[pp][:, t, e:e + 1], acc[pp][:, t, :],
                                                              ALU.mult, ALU.add)
                    last.then_inc(o_added, 1)

                def finish_stats():
                    dve.wait_ge(o_added, E * b)
                    statistics(acc[1 - par], st_o, mv_o, sto_done, mvo_done, prev, xho_ready)

                def finish():
                    dve.wait_ge(xho_ready, prev + 1)
                    dve.wait_ge(gate_end_in, 16 * (prev + 1))
                    nc.vector.tensor_tensor(xh_o[:], xh_o[:], over_tokens(gate_end[:, 0, :]), ALU.mult
                                            ).then_inc(outg_ready, 1)
                    dve.wait_ge(outg_ready, prev + 1)
                    dve.wait_ge(xb2_ready, prev + 1)
                    dve.wait_ge(stored, 16 * prev)
                    nc.vector.tensor_tensor(x_done[:], xh_o[:], x_all[:, prev], ALU.add).then_inc(out_ready, 1)

                def start_b():
                    dve.wait_ge(x0_ready, nxt + 1)
                    statistics(x_all[:, nxt], st_b, mv_b, stb_done, mvb_done, nxt, xhb_ready)

                def select(g):
                    dve.wait_ge(g_filled, 2 * nn + g)
                    for t in range(NT):
                        last = nc.vector.tensor_tensor(
                            sel[:, t], slots[:].unsqueeze(1).to_broadcast([P, E // 2, KSEL]),
                            pos_tok[:, nn, t, 4 * g:4 * g + 4].unsqueeze(2).to_broadcast([P, E // 2, KSEL]),
                            ALU.is_equal)
                    last.then_inc(sel_ready, 1)

                def start_a():
                    statistics(x_all[:, nn], st_a, mv_a, sta_done, mva_done, nn, xha_ready)
                    select(0)

                def split_a():
                    dve.wait_ge(xha_ready, nn + 1)
                    dve.wait_ge(g_filled, 2 * nn)
                    nc.vector.tensor_copy(xha_high[:], xh_a[:]).then_inc(xha_rounded, 1)
                    dve.wait_ge(xha_rounded, nn + 1)
                    nc.vector.tensor_tensor(xha_low[:], xh_a[:], xha_high[:], ALU.subtract).then_inc(xha_split, 1)

                def split_f():
                    dve.wait_ge(hTf_rounded, nxt + 1)
                    nc.vector.tensor_tensor(hTf_low[1 - par][:], hT_f[:], hTf_high[1 - par][:], ALU.subtract
                                            ).then_inc(hTf_split, 1)

                def select_gated(e):
                    if e >= 2 or not (isinstance(nn, int) and nn == 0):
                        dve.wait_ge(t_filled, E * nn + e - 1)
                    for t in range(NT):
                        last = nc.vector.tensor_scalar(gsel[e % 2][:, t, :], slots[:], pos_tok[:, nn, t, e:e + 1],
                                                       probs_tok[:, nn, t, e:e + 1], ALU.is_equal, ALU.mult)
                    last.then_inc(gsel_ready, 1)

                def save_y0(e):
                    dve.wait_ge(y0_filled, E * nn + e + 1)
                    if e >= 2 or not (isinstance(nn, int) and nn == 0):
                        dve.wait_ge(sc_filled, E * nn + e - 1)
                    nc.vector.tensor_copy(y0[e % 2][:], a1[:, 0:D]).then_inc(y0_ready, 1)

                def gate_0():
                    dve.wait_ge(sc_filled, E * (nn + 1))
                    dve.wait_ge(x0_ready, nn)
                    dve.wait_ge(gate0_in, 16 * (nn + 1))
                    nc.vector.tensor_tensor(gated0[:], tokens(a2[:]), over_tokens(gate0[:]), ALU.mult
                                            ).then_inc(gated0_ready, 1)

                def q_negative():
                    dve.wait_ge(qpos_ready, nxt + 1)
                    dve.wait_ge(num_filled, nxt)
                    nc.vector.tensor_scalar(q_exp[:], b0_[:], bq1[:], 0.0, ALU.add, ALU.min).then_inc(qmin_ready, 1)

                def k_negative():
                    dve.wait_ge(uk_filled, nxt + 1)
                    dve.wait_ge(kphi_ready, nxt)
                    nc.vector.tensor_scalar(k_exp[:], b1_[:], 0.0, None, ALU.min).then_inc(kmin_ready, 1)

                def k_features():
                    dve.wait_ge(kexp_ready, nxt + 1)
                    dve.wait_ge(ctx_filled, nxt)
                    nc.vector.scalar_tensor_tensor(k_phi[:].rearrange("p t n -> p (t n)"), b1_[:], 0.0, k_exp[:],
                                                   ALU.max, ALU.add).then_inc(kphi_ready, 1)

                def mask_context():
                    dve.wait_ge(ctx_filled, nxt + 1)
                    dve.wait_ge(num_filled, nxt)
                    nc.vector.tensor_tensor(context[:, 0:P], b1_[:, 0:P], block_mask[:, 0:P], ALU.mult)
                    nc.vector.tensor_scalar(context[:, P:P + H], block_mask[:, P:P + H], b1_[:, P:P + 1], None,
                                            ALU.mult).then_inc(ctx_ready, 1)

                def divide():
                    dve.wait_ge(num_filled, nxt + 1)
                    nc.vector.tensor_scalar(den[:], b1_[:, 0:NT * H], 1e-6, None, ALU.add).then_inc(den_step, 1)
                    dve.wait_ge(den_step, nxt + 1)
                    dve.wait_ge(att1_ready, nxt)
                    nc.vector.reciprocal(den_inv[:], den[:]).then_inc(den_ready, 1)
                    dve.wait_ge(den_ready, nxt + 1)
                    dve.wait_ge(attT1_filled, nxt)
                    nc.vector.tensor_tensor(att1[:].rearrange("p t (h e) -> p (t h) e", e=HD),
                                            b0_[:].rearrange("p (n e) -> p n e", e=HD),
                                            den_inv[:].unsqueeze(2).to_broadcast([P, NT * H, HD]), ALU.mult
                                            ).then_inc(att1_ready, 1)

                def residual_1():
                    dve.wait_ge(o1_filled, nxt + 1)
                    dve.wait_ge(xb1_ready, nxt + 1)
                    nc.vector.tensor_tensor(x_all[:, nxt], tokens(b1_[:]), x_all[:, nxt], ALU.add).then_inc(x1_ready, 1)
                    dve.wait_ge(x1_ready, nxt + 1)
                    statistics(x_all[:, nxt], st_f, mv_f, stf_done, mvf_done, nxt, xhf_ready)

                def shift_logits():
                    dve.wait_ge(l_filled, nxt + 1)
                    v = b1_[:, 0:NT * E].rearrange("p (t e) -> p t e", t=NT)
                    nc.vector.tensor_reduce(lmax[:], v, AX.X, ALU.max).then_inc(l_step, 1)
                    dve.wait_ge(l_step, nxt + 1)
                    dve.wait_ge(lexp_ready, nxt)
                    nc.vector.tensor_tensor(lshift[:], v, lmax[:].unsqueeze(2).to_broadcast([P, NT, E]), ALU.subtract
                                            ).then_inc(lshift_ready, 1)

                def best_two():
                    done = 9 * nxt

                    def step(n, ins):
                        ins.then_inc(top_step, 1)
                        dve.wait_ge(top_step, done + n)

                    def of(ap, axis):
                        return ap.unsqueeze(axis).to_broadcast([P, NT, E, E])

                    dve.wait_ge(lexp_ready, nxt + 1)
                    step(1, nc.vector.tensor_reduce(lsum[:], lexp[:], AX.X, ALU.add))
                    step(2, nc.vector.reciprocal(linv[:], lsum[:]))
                    step(3, nc.vector.tensor_tensor(prob[:], lexp[:], linv[:].unsqueeze(2).to_broadcast([P, NT, E]),
                                                    ALU.mult))
                    nc.vector.tensor_tensor(above[:], of(prob[:], 2), of(prob[:], 3), ALU.is_gt).then_inc(top_step, 1)
                    step(5, nc.vector.tensor_tensor(tied[:], of(prob[:], 2), of(prob[:], 3), ALU.is_equal))
                    step(6, nc.vector.tensor_tensor(tied[:], tied[:], lower[:].unsqueeze(1).to_broadcast([P, NT, E, E]),
                                                    ALU.mult))
                    step(7, nc.vector.tensor_tensor(above[:], above[:], tied[:], ALU.add))
                    step(8, nc.vector.tensor_reduce(ahead[:], above[:], AX.X, ALU.add))
                    step(9, nc.vector.scalar_tensor_tensor(top2[:], ahead[:], 1.5, prob[:], ALU.is_lt, ALU.mult))

                def combine():
                    nc.vector.tensor_reduce(tsum[:], top2[:], AX.X, ALU.add).then_inc(l_sum, 1)
                    dve.wait_ge(l_sum, nxt + 1)
                    nc.vector.reciprocal(tinv[:], tsum[:]).then_inc(l_inv, 1)
                    dve.wait_ge(l_inv, nxt + 1)
                    nc.vector.tensor_tensor(comb[1 - par][:], top2[:], tinv[:].unsqueeze(2).to_broadcast([P, NT, E]),
                                            ALU.mult).then_inc(comb_ready, 1)

                def shared():
                    dve.wait_ge(sh_filled, nxt + 1)
                    dve.wait_ge(acc_ready, nxt)
                    nc.vector.tensor_tensor(sh[:], tokens(b0_[:]), over_tokens(shared_b[:]), ALU.add
                                            ).then_inc(sh_ready, 1)

                def start_acc():
                    dve.wait_ge(shg_ready, nxt + 1)
                    dve.wait_ge(b2_filled, nxt + 1)
                    if it.before:
                        dve.wait_ge(xho_ready, b)
                    nc.vector.scalar_tensor_tensor(acc[1 - par][:], sh[:], 0.5, tokens(b0_[:]), ALU.mult, ALU.add
                                                   ).then_inc(acc_ready, 1)

                work = {q: [] for q in range(Q)}
                if it.before:
                    work[3].append(finish_stats)
                    work[6].append(finish)
                if it.later:
                    work[0].append(start_a)
                    work[1].append(split_a)
                if it.after:
                    for q, f in ((0, start_b), (8, q_negative), (9, k_negative), (11, k_features), (13, mask_context),
                                 (16, divide), (21, residual_1), (26, shift_logits), (27, split_f), (28, best_two), (28, combine),
                                 (28, shared), (31, start_acc)):
                        work[q].append(f)
                if it.later:
                    work[3].append(lambda: select(1))
                    for e in range(E):
                        work[4 + 3 * e].append(lambda e=e: select_gated(e))
                        work[7 + 3 * e].append(lambda e=e: save_y0(e))
                    work[30].append(gate_0)
                for q in range(Q):
                    if q == 3 and it.before:
                        add_expert(prev, E - 1, 1 - par)
                    elif q % 4 == 3 and q > 3 and it.here:
                        add_expert(b, q // 4 - 1, par)
                    for f in work[q]:
                        f()

            pipeline(dve, iteration)

        @block.tensor
        def _(pe):
            pe.wait_ge(rank_ready, 1)
            for t in range(NT):
                last = nc.tensor.transpose(a0[:, B * E * t:B * E * (t + 1)], rank[:, quarter(t)],
                                           ident[0:B * E, 0:B * E])
            last.then_inc(pos_filled, 1)
            pe.wait_ge(pos_ready, 1)
            pe.wait_ge(small_in, 224)
            pe.wait_ge(w0_in, 32)

            def hidden_quarter(b, q, par):
                e, n = q // 4, q % 4
                if q == 0:
                    pe.wait_ge(hTf_split, b + 1)
                    pe.wait_ge(w1_ready, 2)
                if q >= 2 or not (isinstance(b, int) and b == 0):
                    pe.wait_ge(hid1_ready, Q * b + q - 1)
                nc.tensor.matmul(ps_z[q % 2][:], w1_high[:, e, quarter(n)], hTf_high[par][:], start=True, stop=False)
                nc.tensor.matmul(ps_z[q % 2][:], w1_high[:, e, quarter(n)], hTf_low[par][:], start=False, stop=False)
                nc.tensor.matmul(ps_z[q % 2][:], w1_low[:, e, quarter(n)], hTf_high[par][:], start=False, stop=True
                                 ).then_inc(z_filled, 1)

            def outputs(b, e, step):
                if step == 0:
                    pe.wait_ge(w2_in, 16)
                    pe.wait_ge(hid1_ready, Q * b + 4 * (e + 1))
                    pe.wait_ge(o_added, E * b + e)
                for t in ((0,), (1, 2), (3,), ())[step]:
                    for f in range(NF):
                        last = nc.tensor.matmul(ps_o[:, quarter(t)], hid1[e % 2][:, f, quarter(t)], w2_1[:, e, f, :],
                                                start=(f == 0), stop=(f == NF - 1))
                if step == 2:
                    last.then_inc(o_filled, 1)

            def transposes(bank, of, filled):
                for t in range(NT):
                    last = nc.tensor.transpose(bank[:, quarter(t)], of(t), ident[:])
                last.then_inc(filled, 1)

            def by_token(bank, lhs, rhs, width, filled):
                for t in range(NT):
                    last = nc.tensor.matmul(bank[:, width * t:width * (t + 1)], lhs(t), rhs, start=True, stop=True)
                last.then_inc(filled, 1)

            def iteration(it, par):
                b, nxt, nn, prev = it.own, it.own + 1, it.own + 2, it.own - 1

                def gather(g):
                    if g == 0:
                        pe.wait_ge(hid0_ready, E * nn)
                        pe.wait_ge(xha_split, nn + 1)
                    else:
                        pe.wait_ge(y0_ready, E * nn)
                    pe.wait_ge(sel_ready, 2 * nn + g + 1)
                    for t in range(NT):
                        for part in (xha_high, xha_low):
                            last = nc.tensor.matmul((a0, a1)[g][:], part[:, t, :],
                                                    sel[:, t].rearrange("p e k -> p (e k)"),
                                                    start=(t == 0 and part is xha_high),
                                                    stop=(t == NT - 1 and part is xha_low))
                    last.then_inc(g_filled, 1)

                def gated_T(e):
                    pe.wait_ge(gsel_ready, E * nn + e + 1)
                    if e == 0:
                        pe.wait_ge(xin_ready, 2 * nn + 2)
                    else:
                        pe.wait_ge(y0_ready, E * nn + e)
                    transposes(a1, lambda t: gsel[e % 2][:, t, :], t_filled)

                def hidden0(e):
                    pe.wait_ge(xin_ready, 2 * nn + 1 + e // 4)
                    pe.wait_ge(hid0_ready, E * nn + e)
                    for f in range(NF):
                        last = nc.tensor.matmul(a0[:, quarter(f)], w1_0[:, e, quarter(f)], xin[:, e, :],
                                                start=True, stop=True)
                    last.then_inc(z0_filled, 1)

                def output0(e):
                    pe.wait_ge(hid0_ready, E * nn + e + 1)
                    pe.wait_ge(gselT_ready, E * nn + e + 1)
                    for f in range(NF):
                        last = nc.tensor.matmul(a1[:, 0:D], hid0[e % 2][:, f, :], w2_0[:, e, f, :],
                                                start=(f == 0), stop=(f == NF - 1))
                    last.then_inc(y0_filled, 1)

                def scatter(e):
                    pe.wait_ge(y0_ready, E * nn + e + 1)
                    if e == 0:
                        pe.wait_ge(gated0_ready, nn)
                    for t in range(NT):
                        last = nc.tensor.matmul(a2[:, quarter(t)], gselT[e % 2][:, quarter(t)], y0[e % 2][:],
                                                start=(e == 0 and t == 0), stop=(e == E - 1), skip_group_check=True)
                    last.then_inc(sc_filled, 1)

                def norm1_T():
                    pe.wait_ge(xhb_ready, nxt + 1)
                    pe.wait_ge(acc_ready, nxt)
                    transposes(b0_, lambda t: xh_b[:, t, :], hT1_filled)

                def latents():
                    pe.wait_ge(hT1_ready, nxt + 1)
                    pe.wait_ge(combT_ready, nxt)
                    nc.tensor.matmul(b1_[0:R, :], wd[:], hT1[:], start=True, stop=True).then_inc(lat_filled, 1)

                def queries():
                    nc.tensor.matmul(b0_[:], wq1[:], hT1[:], start=True, stop=True).then_inc(q1_filled, 1)

                def keys():
                    pe.wait_ge(lat_ready, nxt + 1)
                    by_token(b1_, lambda t: latent[:, quarter(t)], wu[:, 0:D], D, uk_filled)

                def values():
                    pe.wait_ge(qpos_ready, nxt + 1)
                    pe.wait_ge(qmin_ready, nxt + 1)
                    by_token(b0_, lambda t: latent[:, quarter(t)], wu[:, D:2 * D], D, uv_filled)

                def contexts():
                    pe.wait_ge(kphi_ready, nxt + 1)
                    pe.wait_ge(v1_ready, nxt + 1)
                    for t in range(NT):
                        last = nc.tensor.matmul(b1_[:, 0:D + 1], k_phi[:, t, :], v1[:, t, :],
                                                start=(t == 0), stop=(t == NT - 1))
                    last.then_inc(ctx_filled, 1)

                def attend():
                    pe.wait_ge(ctx_ready, nxt + 1)
                    pe.wait_ge(qphi_ready, nxt + 1)
                    for t in range(NT):
                        nc.tensor.matmul(b0_[:, quarter(t)], q_exp[:, quarter(t)], context[:, 0:P],
                                         start=True, stop=True)
                        last = nc.tensor.matmul(b1_[:, H * t:H * (t + 1)], q_exp[:, quarter(t)], context[:, P:P + H],
                                                start=True, stop=True)
                    last.then_inc(num_filled, 1)

                def att_T():
                    pe.wait_ge(att1_ready, nxt + 1)
                    transposes(b0_, lambda t: att1[:, t, :], attT1_filled)

                def project_o():
                    pe.wait_ge(attT1_ready, nxt + 1)
                    pe.wait_ge(wo1g_ready, nxt + 1)
                    by_token(b1_, lambda t: attT1[:, quarter(t)], wo1_gated[:], D, o1_filled)

                def norm2_T():
                    pe.wait_ge(xhf_ready, nxt + 1)
                    transposes(b0_, lambda t: xh_f[:, t, :], hTf_filled)

                def logits():
                    pe.wait_ge(hTf_ready, nxt + 1)
                    pe.wait_ge(x1_ready, nxt + 1)
                    by_token(b1_, lambda t: hT_f[:, quarter(t)], gate1[:], E, l_filled)

                def shared():
                    by_token(b0_, lambda t: hT_f[:, quarter(t)], shared_w[:], D, sh_filled)

                def comb_T():
                    pe.wait_ge(comb_ready, nxt + 1)
                    for t in range(NT):
                        last = nc.tensor.transpose(b1_[0:E, quarter(t)], comb[1 - par][:, t, :], ident[:])
                    last.then_inc(combT_filled, 1)

                def biases():
                    pe.wait_ge(combT_ready, nxt + 1)
                    pe.wait_ge(sh_ready, nxt + 1)
                    by_token(b0_, lambda t: combT[:, quarter(t)], b2[:], D, b2_filled)

                work = {q: [] for q in range(Q)}
                if it.after:
                    for q, f in ((3, norm1_T), (6, latents), (7, queries), (9, keys), (10, values), (13, contexts),
                                 (16, attend), (19, att_T), (21, project_o), (25, norm2_T), (26, logits),
                                 (27, shared), (30, comb_T), (31, biases)):
                        work[q].append(f)
                if it.later:
                    work[2].append(lambda: gather(0))
                    work[4].append(lambda: gather(1))
                    for e in range(E):
                        work[5 + 3 * e].append(lambda e=e: gated_T(e))
                        work[5 + 3 * e].append(lambda e=e: hidden0(e))
                        work[7 + 3 * e].append(lambda e=e: output0(e))
                        work[8 + 3 * e].append(lambda e=e: scatter(e))
                for q in range(Q):
                    if it.here:
                        hidden_quarter(b, q, par)
                    if q < 4:
                        if it.before:
                            outputs(prev, E - 1, q)
                    elif it.here:
                        outputs(b, q // 4 - 1, q % 4)
                    for f in work[q]:
                        f()

            pipeline(pe, iteration)


def build(nc, io):
    scratch = {"k": nc.dram_tensor("k_parts_dram", (PARTS * HD, H, T), BF16, kind="Internal"),
               "q": nc.dram_tensor("q_parts_dram", (QSLOTS * HD, H, T), BF16, kind="Internal"),
               "gates": nc.dram_tensor("gates_dram", (7, B, D), F32, kind="Internal"),
               "probs": nc.dram_tensor("probs_dram", (B, E, T), F32, kind="Internal")}
    with ExitStack() as ctx:
        shapes = {"x": [P, B, NT, D], "probs": [P, B, NT, E], "mod": [P, 2, 6, B], "scale1": [P, 2, 2, B],
                  "ident": [P, P]}
        keep = {name: ctx.enter_context(nc.sbuf_tensor(name, shape, F32)) for name, shape in shapes.items()}
        held = []
        program_attention(nc, io, keep, scratch, held)
        nc.all_engine_barrier()
        nc.clear_and_free_semaphores(held)
        nc.all_engine_barrier()
        program_experts(nc, io, keep, scratch, [])


def laid_out(v):
    import numpy as np

    eye = np.eye(P, dtype=np.float32)
    head = np.arange(P) // HD
    return {
        "x": v["L0_attn_x"],
        "cT": np.stack([v["L0_c"].T, v["L1_c"].T], 1),
        "wmod": np.stack([v["L0_wmod"], v["L1_wmod"]], 1),
        "ident": eye,
        "wq": v["L0_attn_wq"].transpose(1, 0, 2).reshape(D, P),
        "wk": v["L0_attn_wk"].transpose(1, 0, 2).reshape(D, P),
        "wv": v["L0_attn_wv"].transpose(1, 0, 2).reshape(D, P),
        "bq": v["L0_attn_bq"].reshape(P, 1),
        "bk": v["L0_attn_bk"].reshape(P, 1),
        "bv": v["L0_attn_bv"].reshape(P),
        "vectors": np.stack([v["L0_attn_bo"], v["L1_attn_bo"], v["L1_ffn_gamma"], v["L1_ffn_beta"]]),
        "wo": v["L0_attn_wo"].T,
        "gate_w": v["L0_ffn_gate_w"].T,
        "w1_0": v["L0_ffn_w1"],
        "w2_0": v["L0_ffn_w2"],
        "w1_1": v["L1_ffn_W1"],
        "w2_1": v["L1_ffn_W2"],
        "b1": v["L1_ffn_b1"].reshape(E, NF, P).transpose(2, 0, 1),
        "b2": v["L1_ffn_b2"],
        "wq1": v["L1_attn_Wq"],
        "bq1": v["L1_attn_bq"].reshape(P, 1),
        "wd": v["L1_attn_Wd"],
        "bd": v["L1_attn_bd"].reshape(R, 1),
        "wu": np.concatenate([v["L1_attn_Wu"], v["L1_attn_bu"][None]]).reshape(R + 1, H, 2, HD)
                .transpose(0, 2, 1, 3).reshape(R + 1, 2 * D),
        "wo1": v["L1_attn_Wo"],
        "gate1": v["L1_ffn_gate_W"],
        "shared_w": v["L1_ffn_shared_W"],
        "shared_b": v["L1_ffn_shared_b"],
        "slots": np.arange(1, KSEL + 1, dtype=np.float32),
        "block_mask": np.concatenate([head[:, None] == head[None], head[:, None] == np.arange(H)[None]], 1
                                     ).astype(np.float32),
        "lower": (np.arange(E)[None] < np.arange(E)[:, None]).astype(np.float32),
    }


def kernel(**inputs):
    import numpy as np
    import concourse.bacc as bacc
    from concourse.bass_utils import run_bass_kernel_spmd

    arrays = {f"in_{name}": np.ascontiguousarray(a) for name, a in laid_out(
        {name: np.asarray(a) for name, a in inputs.items()}).items()}
    nc = bacc.Bacc("TRN2", target_bir_lowering=False, num_devices=1)
    io = {name[3:]: nc.dram_tensor(name, a.shape, mybir.dt.from_np(a.dtype), kind="ExternalInput").ap()
          for name, a in arrays.items()}
    io["out"] = nc.dram_tensor("out_x", (B, T, D), F32, kind="ExternalOutput").ap()
    build(nc, io)
    result = run_bass_kernel_spmd(nc, [arrays], core_ids=[0])
    return result.results[0]["out_x"]
```

```python
from contextlib import ExitStack

import concourse.bass as bass
from concourse import mybir

F32 = mybir.dt.float32
BF16 = mybir.dt.bfloat16
F32R = mybir.dt.float32r
ALU = mybir.AluOpType
ACT = mybir.ActivationFunctionType
AX = mybir.AxisListType

P = 128
B, T, D = 8, 512, 128
NT = T // P
H, HD = 16, 8
HG = 4
NG = H // HG
E, F = 8, 512
NF = F // P
KSEL = 2 * T // E
ROUNDS = KSEL // 8
EARLY = (B - 1) * E
EPS = 1e-5
UNITS = H * NT
PARTS = 3
TERMS = PARTS * PARTS
STACK = TERMS * HD
MROW = STACK
R = 32
RING = 16
SBANKS, TBANKS = 3, 2
QSLOTS = 5

SHIFT_A, SCALE_A, GATE_A, SHIFT_B, SCALE_B, GATE_B = range(6)


class Batch:

    def __init__(self, own, before=True, here=True, after=True):
        self.own, self.before, self.here, self.after = own, before, here, after


def as_bf16(bank):
    return bank[:].bitcast(BF16)


def window(tensor, offset, dims):
    return bass.AP(tensor=tensor, offset=offset, ap=dims)


def units_back(u, banks):
    return banks if u >= banks else UNITS + u - max(w for w in range(UNITS) if w % banks == u)


def settle(eng):
    eng.nop(nofuse=True)


def norm(nc, half, xin, mv, rstd, step, bb, out, ready):
    pool = nc.gpsimd

    def over_features(ap):
        return ap.unsqueeze(2).to_broadcast([P, NT, D])

    settle(pool)
    nc.gpsimd.tensor_scalar(rstd[:, 0, :], mv[:, :, 1], EPS, None, ALU.add).then_inc(step, 1)
    nc.gpsimd.tensor_tensor(out[:], xin, over_features(mv[:, :, 0]), ALU.subtract).then_inc(step, 1)
    pool.wait_ge(step, 3 * bb + 1)
    nc.gpsimd.tensor_tensor(rstd[:, 1, :], rstd[:, 0, :], half[:], ALU.pow).then_inc(step, 1)
    pool.wait_ge(step, 3 * bb + 3)
    nc.gpsimd.tensor_tensor(out[:], out[:], over_features(rstd[:, 1, :]), ALU.mult).then_inc(ready, 1)


def take_best(nc, rows, best, found, taken, n):
    if n:
        nc.vector.wait_ge(taken, n)
    nc.vector.max(best, rows[n % 2]).then_inc(found, 1)
    nc.vector.wait_ge(found, n + 1)
    nc.vector.match_replace(out=rows[(n + 1) % 2], in_to_replace=best, in_values=rows[n % 2], imm_value=-1.0
                            ).then_inc(taken, 1)


def rank_taken(nc, rows, is_taken, rank, taken, step, ready):
    nc.vector.wait_ge(taken, ROUNDS)
    nc.vector.tensor_scalar(is_taken, rows[0], 0.0, None, ALU.is_lt).then_inc(step, 1)
    nc.vector.wait_ge(step, 1)
    nc.vector.tensor_tensor_scan(rows[1], is_taken, is_taken, 0.0, ALU.add, ALU.max).then_inc(step, 1)
    nc.vector.wait_ge(step, 2)
    nc.vector.tensor_tensor(rank, rows[1], is_taken, ALU.mult).then_inc(ready, 1)


def scores_of(u, it):
    j = u // (HG * NT)
    if j < NG // 2:
        return it.own, j + NG // 2, it.here
    return it.own + 1, j - NG // 2, it.after


def program_attention(nc, io, keep, scratch, held):
    ctx = ExitStack()
    with ctx:
        def sb(name, shape, dt=F32):
            return ctx.enter_context(nc.sbuf_tensor(name, shape, dt))

        def pb(name, shape, dt=F32):
            return ctx.enter_context(nc.psum_tensor(name, shape, dt))

        def sem(name):
            held.append(nc.alloc_semaphore(name=name))
            return held[-1]

        x_all, probs_tok, pos_tok, mod, scale1, ident = (
            keep["x"], keep["probs"], keep["pos"], keep["mod"], keep["scale1"], keep["ident"])

        wq = sb("wq", [P, P])
        wk = sb("wk", [P, P])
        wv = sb("wv", [P, P])
        wo = sb("wo", [P, P])
        bq = sb("bq", [P, 1])
        bk = sb("bk", [P, 1])
        bv = sb("bv", [P, P])
        gate_w = sb("gate_w", [P, E])
        wmod = sb("wmod", [P, 2, 6 * D])
        gates = sb("gates", [P, 2, B, D])
        cT = sb("cT", [P, 2, B])
        siluT = sb("siluT", [P, 2, B])
        sig = sb("sig", [P, 2, B])
        vectors = sb("vectors", [B, 4, D])
        gsign = sb("gsign", [B, 4, D])
        graw = sb("graw", [B, 4, D])
        gstep = sb("gstep", [B, 4, D])
        gabs = sb("gabs", [B, 4, D])
        gclamp = sb("gclamp", [B, 4, D])
        grow = sb("grow", [B, 7, D])
        ident_b = sb("ident_b", [P, P], BF16)
        ones = sb("ones", [48, T], BF16)
        half = sb("half", [P, NT])
        q_stack = [sb(f"q_stack{i}", [P, H, T], BF16) for i in range(2)]
        k_stack = [sb(f"k_stack{i}", [P, H, T], BF16) for i in range(2)]
        v_ext = [sb(f"v_ext{i}", [P, NT, H, 32]) for i in range(2)]
        probs = sb("p_ring", [P, RING, T])
        hT = sb("hT", [P, T])
        xh1 = sb("xh1", [P, NT, D])
        xh2 = sb("xh2", [P, NT, D])
        st1 = sb("st1", [P, NT, 6])
        mv1 = sb("mv1", [P, NT, 2])
        st2 = sb("st2", [P, NT, 6])
        mv2 = sb("mv2", [P, NT, 2])
        rstd1 = sb("rstd1", [P, 3, NT])
        rstd2 = sb("rstd2", [P, 3, NT])
        q_parts = sb("q_parts", [P, PARTS, T], BF16)
        k_parts = sb("k_parts", [P, PARTS, T], BF16)
        q_rest = sb("q_rest", [P, T])
        k_rest = sb("k_rest", [P, T])
        nmax = sb("nmax", [P, NG, HG * NT])
        m_rest = sb("m_rest", [P, HG * NT])
        m_parts = sb("m_parts", [P, NG, PARTS * HG * NT], BF16)
        m_rows = sb("m_rows", [PARTS * HG * NT, NG, P], BF16)
        att = sb("att", [P, 2, T])
        rec = sb("rec", [P, NG, NT, HG])
        att_tok = sb("att_tok", [P, NT, D])
        attT = sb("attT", [P, T])
        wo_gated = sb("wo_gated", [P, D])
        h2T = sb("h2T", [P, T])
        lg_max = sb("lg_max", [P, NT])
        lg = sb("lg", [P, NT, E])
        lg_exp = sb("lg_exp", [P, NT, E])
        lg_sum = sb("lg_sum", [P, NT])
        lg_inv = sb("lg_inv", [P, NT])
        prob_now = sb("prob_now", [P, NT, E])
        probT = sb("probT", [E, T])

        rows = [sb(f"rows{i}", [EARLY, T])[:] for i in range(2)]
        is_taken = sb("is_taken", [EARLY, T])
        rank = sb("rank", [EARLY, T])
        best = sb("best", [EARLY, 8])

        ps_s = [pb(f"ps_s{i}", [P, T]) for i in range(SBANKS)]
        ps_t = [pb(f"ps_t{i}", [P, T]) for i in range(TBANKS)]
        ps_av = pb("ps_av", [P, T])
        bank_a = pb("bank_a", [P, T])
        bank_b = pb("bank_b", [P, T])

        cT_in = sem("cT_in")
        c_in = sem("c_in")
        wqkv_in = sem("wqkv_in")
        x0_in = sem("x0_in")
        x_in = sem("x_in")
        rest_in = sem("rest_in")
        ones_in = sem("ones_in")
        sig_e = sem("sig_e")
        silu = sem("silu")
        mod_mm = sem("mod_mm")
        mod_ready = sem("mod_ready")
        gate_mm = sem("gate_mm")
        gate_step = sem("gate_step")
        grow_ready = sem("grow_ready")
        grow_out = sem("grow_out")
        gates_in = sem("gates_in")
        consts = sem("consts")
        identb_ready = sem("identb_ready")
        st1_done = sem("st1_done")
        mv1_done = sem("mv1_done")
        r1_step = sem("r1_step")
        xh1_ready = sem("xh1_ready")
        hT_filled = sem("hT_filled")
        hT_ready = sem("hT_ready")
        q_filled = sem("q_filled")
        q1_ready = sem("q1_ready")
        q_rest_ready = sem("q_rest_ready")
        q2_ready = sem("q2_ready")
        q3_ready = sem("q3_ready")
        k_filled = sem("k_filled")
        k1_ready = sem("k1_ready")
        k_rest_ready = sem("k_rest_ready")
        k2_ready = sem("k2_ready")
        k3_ready = sem("k3_ready")
        v_filled = sem("v_filled")
        v_ready = sem("v_ready")
        q_saved = sem("q_saved")
        k_saved = sem("k_saved")
        stack_in = [sem(f"stack_in{j}") for j in range(NG)]
        s_filled = sem("s_filled")
        max_done = sem("max_done")
        t_filled = sem("t_filled")
        exp_done = sem("exp_done")
        av_done = sem("av_done")
        av_saved = sem("av_saved")
        m_step = sem("m_step")
        m_parts_ready = [sem(f"m_parts_ready{j}") for j in range(NG)]
        m_filled = [sem(f"m_filled{j}") for j in range(NG)]
        m_rows_ready = [sem(f"m_rows_ready{j}") for j in range(NG)]
        m_in = [sem(f"m_in{j}") for j in range(NG)]
        avT_filled = [sem(f"avT_filled{j}") for j in range(NG)]
        rec_done = [sem(f"rec_done{j}") for j in range(NG)]
        avT_read = [sem(f"avT_read{j}") for j in range(NG)]
        attT_filled = sem("attT_filled")
        attT_ready = sem("attT_ready")
        wog_ready = sem("wog_ready")
        xbias_ready = sem("xbias_ready")
        o_filled = sem("o_filled")
        x_ready = sem("x_ready")
        st2_done = sem("st2_done")
        mv2_done = sem("mv2_done")
        r2_step = sem("r2_step")
        xh2_ready = sem("xh2_ready")
        h2T_filled = sem("h2T_filled")
        h2T_ready = sem("h2T_ready")
        lg_filled = sem("lg_filled")
        lg_step = sem("lg_step")
        lg_ready = sem("lg_ready")
        lg_exp_ready = sem("lg_exp_ready")
        prob_inv = sem("prob_inv")
        prob_ready = sem("prob_ready")
        prob_kept = sem("prob_kept")
        pT_filled = sem("pT_filled")
        probT_ready = sem("probT_ready")
        probT_out = sem("probT_out")
        rows_in = sem("rows_in")
        best_found = sem("best_found")
        best_taken = sem("best_taken")
        rank_step = sem("rank_step")
        rank_ready = sem("rank_ready")
        pos_filled = sem("pos_filled")
        pos_ready = sem("pos_ready")

        block = ctx.enter_context(nc.Block())

        def pipeline(eng, iteration):
            iteration(Batch(-1, before=False, here=False), 1)
            iteration(Batch(0, before=False), 0)
            iteration(Batch(1), 1)
            with eng.Fori(0, (B - 4) // 2) as i:
                iteration(Batch(2 * i + 2), 0)
                iteration(Batch(2 * i + 3), 1)
            iteration(Batch(B - 2), B % 2)
            iteration(Batch(B - 1, after=False), (B - 1) % 2)
            iteration(Batch(B, here=False, after=False), B % 2)

        def tokens(ap):
            return ap.rearrange("p (t n) -> p t n", t=NT)

        @block.sync
        def _(sp):
            sp.dma_start(cT[:], io["cT"]).then_inc(cT_in, 16)
            sp.dma_start(x_all[:, 0], io["x"][0].rearrange("(t p) d -> p t d", p=P)).then_inc(x0_in, 16)
            sp.dma_start(wmod[:], io["wmod"]).then_inc(c_in, 16)
            sp.dma_start(ident[:], io["ident"]).then_inc(c_in, 16)
            for tile, name in ((wq, "wq"), (wk, "wk"), (wv, "wv"), (bq, "bq"), (bk, "bk")):
                sp.dma_start(tile[:], io[name]).then_inc(wqkv_in, 16)
            sp.dma_start(bv[:], io["bv"].partition_broadcast(P)).then_inc(wqkv_in, 16)
            sp.dma_start(vectors[:], io["vectors"].partition_broadcast(B)).then_inc(rest_in, 16)
            sp.dma_start(wo[:], io["wo"]).then_inc(rest_in, 16)
            sp.dma_start(gate_w[:], io["gate_w"]).then_inc(rest_in, 16)
            sp.dma_start(x_all[:, 1:B], io["x"][1:B].rearrange("b (t p) d -> p b t d", p=P)).then_inc(x_in, 16)
            sp.wait_ge(consts, 1)
            for i in range(2):
                sp.dma_start(k_stack[i][MROW:MROW + PARTS], ones[:]).then_inc(ones_in, 16)

            def move_maxima(bb, j, par):
                sp.wait_ge(m_rows_ready[j], bb + 1)
                sp.dma_start(q_stack[par][MROW:MROW + PARTS, HG * j:HG * (j + 1), :],
                             m_rows[:, j, :]).then_inc(m_in[j], 16)

            def save_parts(parts, ready, saved, dram, slots, bb):
                for j in range(NG):
                    sp.wait_ge(stack_in[j], 32 * bb)
                    settle(sp)
                for c in range(PARTS):
                    sp.wait_ge(ready[c], bb + 1)
                    for slot in range(c, slots, PARTS):
                        sp.dma_start(dram.ap()[slot * HD:(slot + 1) * HD].rearrange("e h t -> h e t"),
                                     parts[:, c, :]).then_inc(saved, 16)

            def iteration(it, par):
                b, nxt, prev = it.own, it.own + 1, it.own - 1
                if it.here:
                    move_maxima(b, 1, par)
                if it.after:
                    save_parts(k_parts, (k1_ready, k2_ready, k3_ready), k_saved, scratch["k"], PARTS, nxt)
                    save_parts(q_parts, (q1_ready, q2_ready, q3_ready), q_saved, scratch["q"], QSLOTS, nxt)
                    if it.before:
                        sp.wait_ge(t_filled, UNITS * b)
                        settle(sp)
                    sp.wait_ge(k_saved, 16 * PARTS * (nxt + 1))
                    settle(sp)
                    sp.wait_ge(q_saved, 16 * QSLOTS * (nxt + 1))
                    settle(sp)
                    for j in range(NG):
                        n = HG * T
                        sp.dma_start(k_stack[1 - par][0:STACK, HG * j:HG * (j + 1), :],
                                     window(scratch["k"], n * j, [[0, PARTS], [H * T, PARTS * HD], [1, n]])
                                     ).then_inc(stack_in[j], 16)
                        sp.dma_start(q_stack[1 - par][0:STACK, HG * j:HG * (j + 1), :],
                                     window(scratch["q"], n * j, [[HD * H * T, PARTS], [H * T, PARTS * HD], [1, n]])
                                     ).then_inc(stack_in[j], 16)
                if not it.here and it.after:
                    sp.wait_ge(grow_ready, 7)
                    sp.dma_start(scratch["gates"].ap().rearrange("k b d -> b k d"), grow[:]).then_inc(grow_out, 16)
                    sp.wait_ge(grow_out, 16)
                    sp.dma_start(gates[:], window(scratch["gates"], 0, [[0, P], [1, 2 * B * D]])).then_inc(gates_in, 16)
                if it.here:
                    move_maxima(b, 2, par)
                    move_maxima(b, 3, par)
                if it.before:
                    sp.wait_ge(probT_ready, prev + 1)
                    sp.dma_start(scratch["probs"].ap()[prev], probT[:]).then_inc(probT_out, 16)
                if it.here and not it.after:
                    sp.wait_ge(probT_out, 16 * (B - 1))
                    sp.dma_start(rows[0], scratch["probs"].ap()[0:B - 1].rearrange("b e t -> (b e) t")
                                 ).then_inc(rows_in, 16)
                if it.after:
                    move_maxima(nxt, 0, 1 - par)

            pipeline(sp, iteration)
            sp.wait_ge(probT_out, 16 * B)

        @block.gpsimd
        def _(pool):
            nc.gpsimd.memset(ones[:], 1.0).then_inc(consts, 1)
            nc.gpsimd.memset(half[:], -0.5).then_inc(consts, 1)
            for i in range(2):
                nc.gpsimd.memset(v_ext[i][:], 0.0).then_inc(consts, 1)
                pool.wait_ge(consts, 3 + 2 * i)
                nc.gpsimd.memset(v_ext[i][:, :, :, HD:HD + 1], 1.0).then_inc(consts, 1)

            def split(rest, rest_ready, parts, second, third, saved, slots, bb):
                pool.wait_ge(rest_ready, bb + 1)
                pool.wait_ge(saved, 16 * slots * bb)
                settle(pool)
                nc.gpsimd.tensor_copy(parts[:, 1, :], rest[:]).then_inc(second, 1)
                pool.wait_ge(second, bb + 1)
                nc.gpsimd.tensor_tensor(parts[:, 2, :], rest[:], parts[:, 1, :], ALU.subtract).then_inc(third, 1)

            def maxima(bb, j):
                done = 3 * (NG * bb + j)
                pool.wait_ge(max_done, UNITS * bb + HG * NT * (j + 1))
                pool.wait_ge(m_filled[j], bb)
                parts = m_parts[:, j, :].rearrange("p (c n) -> p c n", c=PARTS)
                settle(pool)
                nc.gpsimd.tensor_copy(parts[:, 0, :], nmax[:, j, :]).then_inc(m_step, 1)
                pool.wait_ge(m_step, done + 1)
                nc.gpsimd.tensor_tensor(m_rest[:], nmax[:, j, :], parts[:, 0, :], ALU.subtract).then_inc(m_step, 1)
                pool.wait_ge(m_step, done + 2)
                settle(pool)
                nc.gpsimd.tensor_copy(parts[:, 1, :], m_rest[:]).then_inc(m_step, 1)
                pool.wait_ge(m_step, done + 3)
                nc.gpsimd.tensor_tensor(parts[:, 2, :], m_rest[:], parts[:, 1, :], ALU.subtract
                                        ).then_inc(m_parts_ready[j], 1)

            def iteration(it, par):
                b, nxt, prev = it.own, it.own + 1, it.own - 1
                if it.after:
                    pool.wait_ge(mv1_done, nxt + 1)
                    pool.wait_ge(hT_filled, nxt)
                    norm(nc, half, x_all[:, nxt], mv1, rstd1, r1_step, nxt, xh1, xh1_ready)
                if it.here:
                    maxima(b, 1)
                if it.after:
                    split(k_rest, k_rest_ready, k_parts, k2_ready, k3_ready, k_saved, PARTS, nxt)
                    split(q_rest, q_rest_ready, q_parts, q2_ready, q3_ready, q_saved, QSLOTS, nxt)
                if it.before:
                    pool.wait_ge(gates_in, 16)
                    pool.wait_ge(rest_in, 48)
                    pool.wait_ge(o_filled, prev)
                    nc.gpsimd.tensor_tensor(wo_gated[:], wo[:], gates[:, 0, prev, :], ALU.mult).then_inc(wog_ready, 1)
                    for t in range(NT):
                        last = nc.gpsimd.tensor_tensor(x_all[:, prev, t, :], x_all[:, prev, t, :],
                                                       gates[:, 1, prev, :], ALU.add)
                    last.then_inc(xbias_ready, 1)
                if it.here:
                    maxima(b, 2)
                if it.before:
                    pool.wait_ge(mv2_done, prev + 1)
                    pool.wait_ge(h2T_filled, prev)
                    norm(nc, half, x_all[:, prev], mv2, rstd2, r2_step, prev, xh2, xh2_ready)
                if it.here:
                    maxima(b, 3)
                if it.before:
                    pool.wait_ge(prob_ready, prev + 1)
                    settle(pool)
                    nc.gpsimd.tensor_copy(probs_tok[:, prev], prob_now[:]).then_inc(prob_kept, 1)
                if it.after:
                    maxima(nxt, 0)

            pipeline(pool, iteration)

        @block.scalar
        def _(act):
            act.wait_ge(cT_in, 16)
            nc.scalar.activation(sig[:], cT[:], ACT.Exp, scale=-1.0).then_inc(sig_e, 1)

            def exponential(b, u):
                act.wait_ge(t_filled, UNITS * b + u + 1)
                if u % HG == 0 and not (isinstance(b, int) and b == 0 and u < RING):
                    act.wait_ge(av_done, H * b + (u - RING) // HG + 1)
                nc.scalar.activation(probs[:, u % RING, :], ps_t[u % TBANKS][:], ACT.Exp, scale=HD ** -0.5
                                     ).then_inc(exp_done, 1)

            def save_av(b, j):
                act.wait_ge(av_done, H * b + NT * (j + 1))
                if j >= 2:
                    act.wait_ge(avT_filled[j - 2], b + 1)
                else:
                    act.wait_ge(avT_filled[j + 2], b)
                nc.scalar.copy(att[:, j % 2, :], ps_av[:]).then_inc(av_saved, 1)

            def save_maxima(bb, j, bank):
                act.wait_ge(m_filled[j], bb + 1)
                act.wait_ge(m_in[j], 16 * bb)
                n = PARTS * HG * NT
                nc.scalar.copy(m_rows[:, j, :], as_bf16(bank)[0:n, 0:P]).then_inc(m_rows_ready[j], 1)

            def iteration(it, par):
                b, nxt, prev = it.own, it.own + 1, it.own - 1

                def shift_h():
                    act.wait_ge(hT_filled, nxt + 1)
                    act.wait_ge(v_filled, nxt)
                    act.wait_ge(mod_ready, 3)
                    nc.scalar.activation(hT[:], bank_a[:], ACT.Identity, scale=scale1[:, 0, 0, bass.ds(nxt, 1)],
                                         bias=mod[:, 0, SHIFT_A, bass.ds(nxt, 1)]).then_inc(hT_ready, 1)

                def first_part(which):
                    filled, saved, slots, parts, bank, bias, ready = {
                        "q": (q_filled, q_saved, QSLOTS, q_parts, bank_a, bq, q1_ready),
                        "k": (k_filled, k_saved, PARTS, k_parts, bank_b, bk, k1_ready)}[which]
                    act.wait_ge(filled, nxt + 1)
                    act.wait_ge(saved, 16 * slots * nxt)
                    act.wait_ge(wqkv_in, 96)
                    nc.scalar.activation(parts[:, 0, :], bank[:], ACT.Identity, bias=bias[:]).then_inc(ready, 1)

                def save_attT():
                    act.wait_ge(attT_filled, prev + 1)
                    act.wait_ge(o_filled, prev)
                    nc.scalar.copy(attT[:], bank_b[:]).then_inc(attT_ready, 1)

                def shift_h2():
                    act.wait_ge(h2T_filled, prev + 1)
                    act.wait_ge(lg_filled, prev)
                    nc.scalar.activation(h2T[:], bank_b[:], ACT.Identity, scale=scale1[:, 0, 1, bass.ds(prev, 1)],
                                         bias=mod[:, 0, SHIFT_B, bass.ds(prev, 1)]).then_inc(h2T_ready, 1)

                def exp_logits():
                    act.wait_ge(lg_ready, prev + 1)
                    act.wait_ge(prob_ready, prev)
                    nc.scalar.activation(lg_exp[:], lg[:], ACT.Exp).then_inc(lg_exp_ready, 1)

                def save_probT():
                    act.wait_ge(pT_filled, prev + 1)
                    act.wait_ge(probT_out, 16 * prev)
                    nc.scalar.copy(probT[:], bank_b[0:E, :]).then_inc(probT_ready, 1)

                work = {}
                if it.before:
                    work |= {3: lambda: save_av(prev, 3), 17: save_attT, 30: shift_h2, 37: exp_logits, 46: save_probT}
                if it.here:
                    work |= {7: lambda: save_maxima(b, 1, bank_b), 22: lambda: save_maxima(b, 2, bank_b),
                             38: lambda: save_maxima(b, 3, bank_b), 20: lambda: save_av(b, 0),
                             35: lambda: save_av(b, 1), 51: lambda: save_av(b, 2)}
                if it.after:
                    work |= {8: shift_h, 10: lambda: first_part("k"), 13: lambda: first_part("q"),
                             57: lambda: save_maxima(nxt, 0, bank_a)}
                for u in range(UNITS):
                    if it.here:
                        exponential(b, u)
                    if u in work:
                        work[u]()

            pipeline(act, iteration)

        @block.vector
        def _(dve):
            dve.wait_ge(sig_e, 1)
            nc.vector.tensor_scalar(sig[:], sig[:], 1.0, None, ALU.add).then_inc(silu, 1)
            dve.wait_ge(silu, 1)
            nc.vector.reciprocal(sig[:], sig[:]).then_inc(silu, 1)
            dve.wait_ge(silu, 2)
            nc.vector.tensor_tensor(siluT[:], cT[:], sig[:], ALU.mult).then_inc(silu, 1)
            dve.wait_ge(c_in, 32)
            nc.vector.tensor_copy(ident_b[:], ident[:]).then_inc(identb_ready, 1)

            def statistics(xin, st, mv, st_done, mv_done, bb):
                settle(dve)
                for t in range(NT):
                    last = nc.vector.bn_stats(st[:, t, :], xin[:, t, :])
                last.then_inc(st_done, 1)
                dve.wait_ge(st_done, bb + 1)
                settle(dve)
                for t in range(NT):
                    last = nc.vector.bn_aggr(mv[:, t, :], st[:, t, :])
                last.then_inc(mv_done, 1)

            def maximum(bs, js, v, u):
                dve.wait_ge(s_filled, UNITS * bs + HG * NT * js + v + 1)
                if v == 0:
                    dve.wait_ge(m_parts_ready[js], bs)
                n = (v % HG) * NT + v // HG
                nc.vector.tensor_reduce(nmax[:, js, n:n + 1], ps_s[u % SBANKS][:], AX.X, ALU.max, negate=True
                                        ).then_inc(max_done, 1)

            def mod_vectors():
                dve.wait_ge(mod_mm, 1)
                v = bank_b[:, 0:12 * B].rearrange("p (l c b) -> p l c b", l=2, c=6)
                nc.vector.tensor_copy(mod[:], v).then_inc(mod_ready, 1)
                nc.vector.tensor_scalar(scale1[:, :, 0, :], v[:, :, SCALE_A, :], 1.0, None, ALU.add
                                        ).then_inc(mod_ready, 1)
                nc.vector.tensor_scalar(scale1[:, :, 1, :], v[:, :, SCALE_B, :], 1.0, None, ALU.add
                                        ).then_inc(mod_ready, 1)

            def gate_rows():
                dve.wait_ge(gate_mm, 1)
                v = bank_b[0:B, :].rearrange("p (k d) -> p k d", k=4)
                nc.vector.tensor_copy(graw[:], v).then_inc(gate_step, 1)
                nc.vector.tensor_scalar(gstep[:], v, 0.0, 2.0, ALU.is_ge, ALU.mult).then_inc(gate_step, 1)
                dve.wait_ge(gate_step, 2)
                nc.vector.scalar_tensor_tensor(gabs[:], graw[:], -1.0, graw[:], ALU.mult, ALU.max
                                               ).then_inc(gate_step, 1)
                nc.vector.tensor_scalar(gsign[:], gstep[:], -1.0, None, ALU.add).then_inc(gate_step, 1)
                dve.wait_ge(gate_step, 4)
                nc.vector.scalar_tensor_tensor(gclamp[:], gabs[:], 0.25, gsign[:], ALU.max, ALU.mult
                                               ).then_inc(gate_step, 1)
                dve.wait_ge(gate_step, 5)
                dve.wait_ge(rest_in, 48)
                for to, of, by in ((0, 0, None), (1, 0, 0), (2, 1, None), (3, 2, None), (4, 2, 1), (5, 3, 2),
                                   (6, 3, 3)):
                    if by is None:
                        nc.vector.tensor_copy(grow[:, to, :], gclamp[:, of, :]).then_inc(grow_ready, 1)
                    else:
                        nc.vector.tensor_tensor(grow[:, to, :], gclamp[:, of, :], vectors[:, by, :], ALU.mult
                                                ).then_inc(grow_ready, 1)

            def iteration(it, par):
                b, nxt, prev = it.own, it.own + 1, it.own - 1

                def rest(which):
                    bank, bias, parts, rst, first, ready, third = {
                        "q": (bank_a, bq, q_parts, q_rest, q1_ready, q_rest_ready, q3_ready),
                        "k": (bank_b, bk, k_parts, k_rest, k1_ready, k_rest_ready, k3_ready)}[which]
                    dve.wait_ge(first, nxt + 1)
                    dve.wait_ge(third, nxt)
                    nc.vector.scalar_tensor_tensor(rst[:], bank[:], bias[:], parts[:, 0, :], ALU.add, ALU.subtract
                                                   ).then_inc(ready, 1)

                def values():
                    dve.wait_ge(v_filled, nxt + 1)
                    if it.before:
                        dve.wait_ge(av_done, H * b)
                    dve.wait_ge(consts, 6)
                    heads = bv[:].rearrange("p (h e) -> p h e", h=H).unsqueeze(1).to_broadcast([P, NT, H, HD])
                    nc.vector.tensor_tensor(v_ext[1 - par][:, :, :, 0:HD],
                                            bank_a[:].rearrange("p (t h e) -> p t h e", t=NT, h=H), heads,
                                            ALU.add).then_inc(v_ready, 1)

                def normalise(bb, j, bank):
                    dve.wait_ge(avT_filled[j], bb + 1)
                    v = bank[:].rearrange("p (t g n) -> p t g n", t=NT, g=HG)
                    dve.wait_ge(avT_read[j], bb)
                    nc.vector.reciprocal(rec[:, j], v[:, :, :, HD]).then_inc(rec_done[j], 1)
                    dve.wait_ge(rec_done[j], bb + 1)
                    if j == 0:
                        dve.wait_ge(attT_filled, bb)
                    out = att_tok[:, :, HG * HD * j:HG * HD * (j + 1)].rearrange("p t (g e) -> p t g e", g=HG)
                    nc.vector.tensor_tensor(out, v[:, :, :, 0:HD], rec[:, j].unsqueeze(3).to_broadcast([P, NT, HG, HD]),
                                            ALU.mult).then_inc(avT_read[j], 1)

                def residual():
                    dve.wait_ge(o_filled, prev + 1)
                    dve.wait_ge(xbias_ready, prev + 1)
                    nc.vector.tensor_tensor(x_all[:, prev], tokens(bank_a[:]), x_all[:, prev], ALU.add
                                            ).then_inc(x_ready, 1)
                    dve.wait_ge(x_ready, prev + 1)
                    dve.wait_ge(xh2_ready, prev)
                    statistics(x_all[:, prev], st2, mv2, st2_done, mv2_done, prev)

                def logits():
                    dve.wait_ge(lg_filled, prev + 1)
                    v = bank_a[:, 0:NT * E].rearrange("p (t e) -> p t e", t=NT)
                    nc.vector.tensor_reduce(lg_max[:], v, AX.X, ALU.max).then_inc(lg_step, 1)
                    dve.wait_ge(lg_step, 2 * prev + 1)
                    dve.wait_ge(lg_exp_ready, prev)
                    nc.vector.tensor_tensor(lg[:], v, lg_max[:].unsqueeze(2).to_broadcast([P, NT, E]), ALU.subtract
                                            ).then_inc(lg_ready, 1)

                def router():
                    dve.wait_ge(lg_exp_ready, prev + 1)
                    nc.vector.tensor_reduce(lg_sum[:], lg_exp[:], AX.X, ALU.add).then_inc(lg_step, 1)
                    dve.wait_ge(lg_step, 2 * prev + 2)
                    nc.vector.reciprocal(lg_inv[:], lg_sum[:]).then_inc(prob_inv, 1)
                    dve.wait_ge(prob_inv, prev + 1)
                    dve.wait_ge(pT_filled, prev)
                    dve.wait_ge(prob_kept, prev)
                    nc.vector.tensor_tensor(prob_now[:], lg_exp[:], lg_inv[:].unsqueeze(2).to_broadcast([P, NT, E]),
                                            ALU.mult).then_inc(prob_ready, 1)

                if it.after:
                    if not it.here:
                        dve.wait_ge(x0_in, 16)
                    elif not it.before:
                        dve.wait_ge(x_in, 16)
                    dve.wait_ge(xh1_ready, nxt)
                    statistics(x_all[:, nxt], st1, mv1, st1_done, mv1_done, nxt)
                work = {}
                if it.after and not it.here:
                    work |= {0: mod_vectors, 19: gate_rows}
                if it.before:
                    work |= {8: lambda: normalise(prev, 3, bank_b), 20: residual, 33: logits, 40: router}
                if it.here:
                    work |= {25: lambda: normalise(b, 0, bank_a), 43: lambda: normalise(b, 1, bank_a),
                             59: lambda: normalise(b, 2, bank_b)}
                if it.after:
                    work |= {10: lambda: rest("k"), 14: lambda: rest("q"), 17: values}
                rounds = {}
                if it.here and not it.after:
                    rounds = {50: range(0, 2), 62: range(2, 5)}
                elif not it.here and it.before:
                    rounds = {3: range(5, 6), 15: range(6, 8), 28: range(8, 14), 37: range(14, 15),
                              50: range(15, ROUNDS)}
                for u in range(UNITS):
                    bs, js, there = scores_of(u, it)
                    if there:
                        maximum(bs, js, u % (HG * NT), u)
                    if u in work:
                        work[u]()
                    for n in rounds.get(u, ()):
                        if n == 0:
                            dve.wait_ge(rows_in, 16)
                        take_best(nc, rows, best[:], best_found, best_taken, n)
                if not it.here and it.before:
                    rank_taken(nc, rows, is_taken[:], rank[:], best_taken, rank_step, rank_ready)
                    dve.wait_ge(pos_filled, 1)
                    nc.vector.tensor_copy(
                        pos_tok[:, 0:B - 1], ps_s[0][:, 0:NT * EARLY].rearrange("p (t b e) -> p b t e", t=NT, b=B - 1)
                    ).then_inc(pos_ready, 1)

            pipeline(dve, iteration)

        @block.tensor
        def _(pe):
            def quarter(t):
                return slice(P * t, P * (t + 1))

            pe.wait_ge(c_in, 32)
            pe.wait_ge(silu, 3)
            for l in range(2):
                for c in range(6):
                    n = (6 * l + c) * B
                    last = nc.tensor.matmul(bank_b[:, n:n + B], wmod[:, l, c * D:(c + 1) * D], siluT[:, l, :],
                                            start=True, stop=True)
            last.then_inc(mod_mm, 1)

            def score(bs, js, v, u, par):
                if v == 0:
                    pe.wait_ge(stack_in[js], 32 * (bs + 1))
                done = UNITS * bs + HG * NT * js + v
                back = units_back(u, SBANKS)
                if not (isinstance(done, int) and done < back):
                    pe.wait_ge(max_done, done - back + 1)
                h, t = HG * js + v % HG, v // HG
                nc.tensor.matmul(ps_s[u % SBANKS][:], q_stack[par][0:STACK, h, quarter(t)], k_stack[par][0:STACK, h, :],
                                 start=True, stop=True).then_inc(s_filled, 1)

            def score_t(b, u, par):
                j, t, g = u // (HG * NT), u // HG % NT, u % HG
                if u % (HG * NT) == 0:
                    pe.wait_ge(m_in[j], 16 * (b + 1))
                    pe.wait_ge(ones_in, 32)
                if u >= TBANKS or not (isinstance(b, int) and b == 0):
                    pe.wait_ge(exp_done, UNITS * b + u - units_back(u, TBANKS) + 1)
                h = HG * j + g
                nc.tensor.matmul(ps_t[u % TBANKS][:], k_stack[par][0:STACK + PARTS, h, quarter(t)],
                                 q_stack[par][0:STACK + PARTS, h, :], start=True, stop=True).then_inc(t_filled, 1)

            def weigh(b, k, par):
                j, t = k // NT, k % NT
                pe.wait_ge(exp_done, UNITS * b + HG * (k + 1))
                pe.wait_ge(v_ready, b + 1)
                if t == 0:
                    pe.wait_ge(av_saved, NG * b + j)
                for g in range(HG):
                    last = nc.tensor.matmul(ps_av[32 * g:32 * (g + 1), :], v_ext[par][:, t, HG * j + g, :],
                                            probs[:, (HG * k + g) % RING, :], start=(t == 0), stop=(t == NT - 1))
                last.then_inc(av_done, 1)

            def transposes(bank, of, filled):
                for t in range(NT):
                    last = nc.tensor.transpose(bank[:, quarter(t)], of(t), ident[:])
                last.then_inc(filled, 1)

            def iteration(it, par):
                b, nxt, prev = it.own, it.own + 1, it.own - 1

                def free(*choices):
                    for there, s, n in choices:
                        if there:
                            pe.wait_ge(s, n)
                            return

                def norm_T():
                    pe.wait_ge(xh1_ready, nxt + 1)
                    free((it.here, m_rows_ready[0], b + 1))
                    transposes(bank_a, lambda t: xh1[:, t, :], hT_filled)

                def project_k():
                    pe.wait_ge(hT_ready, nxt + 1)
                    pe.wait_ge(wqkv_in, 96)
                    free((it.before, avT_read[3], prev + 1), (it.here, m_rows_ready[1], b + 1), (True, mod_ready, 3))
                    nc.tensor.matmul(bank_b[:], wk[:], hT[:], start=True, stop=True).then_inc(k_filled, 1)

                def project_q():
                    pe.wait_ge(hT_ready, nxt + 1)
                    nc.tensor.matmul(bank_a[:], wq[:], hT[:], start=True, stop=True).then_inc(q_filled, 1)

                def project_v():
                    free((True, q_rest_ready, nxt + 1))
                    for t in range(NT):
                        last = nc.tensor.matmul(bank_a[:, quarter(t)], hT[:, quarter(t)], wv[:], start=True, stop=True)
                    last.then_inc(v_filled, 1)

                def gate_products():
                    free((True, k_rest_ready, nxt + 1))
                    for k, (l, c) in enumerate(((0, GATE_A), (0, GATE_B), (1, GATE_A), (1, GATE_B))):
                        last = nc.tensor.matmul(bank_b[0:B, k * D:(k + 1) * D], siluT[:, l, :],
                                                wmod[:, l, c * D:(c + 1) * D], start=True, stop=True)
                    last.then_inc(gate_mm, 1)

                def heads_T(bb, j, bank, *choices):
                    free(*choices)
                    pe.wait_ge(av_saved, NG * bb + j + 1)
                    transposes(bank, lambda t: att[:, j % 2, quarter(t)], avT_filled[j])

                def maxima_T(bb, j, bank, *choices):
                    free(*choices)
                    pe.wait_ge(m_parts_ready[j], bb + 1)
                    pe.wait_ge(identb_ready, 1)
                    settle(pe)
                    n = PARTS * HG * NT
                    nc.tensor.transpose(as_bf16(bank)[0:n, 0:P], m_parts[:, j, :], ident_b[:]).then_inc(m_filled[j], 1)

                def tokens_T():
                    pe.wait_ge(avT_read[3], prev + 1)
                    free((it.after, k_rest_ready, nxt + 1))
                    transposes(bank_b, lambda t: att_tok[:, t, :], attT_filled)

                def project_o():
                    pe.wait_ge(attT_ready, prev + 1)
                    pe.wait_ge(wog_ready, prev + 1)
                    free((it.after, v_ready, nxt + 1), (it.here, m_rows_ready[0], b + 1), (True, avT_read[1], prev + 1))
                    for t in range(NT):
                        last = nc.tensor.matmul(bank_a[:, quarter(t)], attT[:, quarter(t)], wo_gated[:],
                                                start=True, stop=True)
                    last.then_inc(o_filled, 1)

                def norm2_T():
                    pe.wait_ge(xh2_ready, prev + 1)
                    free((it.here, m_rows_ready[2], b + 1), (True, attT_ready, prev + 1))
                    transposes(bank_b, lambda t: xh2[:, t, :], h2T_filled)

                def logits():
                    pe.wait_ge(h2T_ready, prev + 1)
                    free((it.here, avT_read[0], b + 1), (True, x_ready, prev + 1))
                    for t in range(NT):
                        last = nc.tensor.matmul(bank_a[:, E * t:E * (t + 1)], h2T[:, quarter(t)], gate_w[:],
                                                start=True, stop=True)
                    last.then_inc(lg_filled, 1)

                def probs_T():
                    pe.wait_ge(prob_ready, prev + 1)
                    free((it.here, m_rows_ready[3], b + 1), (True, h2T_ready, prev + 1))
                    for t in range(NT):
                        last = nc.tensor.transpose(bank_b[0:E, quarter(t)], prob_now[:, t, :], ident[:])
                    last.then_inc(pT_filled, 1)

                work = {}
                if it.after and not it.here:
                    work |= {17: gate_products}
                if it.before:
                    work |= {8: lambda: heads_T(prev, 3, bank_b, (it.here, m_rows_ready[1], b + 1),
                                                (True, avT_read[2], prev + 1)),
                             17: tokens_T, 20: project_o, 30: norm2_T, 33: logits, 45: probs_T}
                if it.here:
                    work |= {6: lambda: maxima_T(b, 1, bank_b, (it.before, avT_read[2], b), (True, gate_step, 2)),
                             21: lambda: maxima_T(b, 2, bank_b, (it.before, attT_ready, prev + 1),
                                                  (True, k_rest_ready, nxt + 1)),
                             26: lambda: heads_T(b, 0, bank_a, (it.before, x_ready, prev + 1),
                                                 (True, v_ready, nxt + 1)),
                             36: lambda: maxima_T(b, 3, bank_b, (it.before, h2T_ready, prev + 1),
                                                  (True, m_rows_ready[2], b + 1)),
                             41: lambda: heads_T(b, 1, bank_a, (it.before, lg_ready, prev + 1),
                                                 (True, avT_read[0], b + 1)),
                             57: lambda: heads_T(b, 2, bank_b, (it.before, probT_ready, prev + 1),
                                                 (True, m_rows_ready[3], b + 1))}
                if it.after:
                    work |= {4: norm_T, 9: project_k, 10: project_q, 15: project_v,
                             53: lambda: maxima_T(nxt, 0, bank_a, (it.here, avT_read[1], b + 1),
                                                  (True, v_ready, nxt + 1))}
                for u in range(UNITS):
                    bs, js, there = scores_of(u, it)
                    if there:
                        score(bs, js, u % (HG * NT), u, par if js >= NG // 2 else 1 - par)
                    if it.here:
                        score_t(b, u, par)
                    if u == HG - 1 and it.before:
                        weigh(prev, H - 1, 1 - par)
                    elif u % HG == HG - 1 and u >= HG and it.here:
                        weigh(b, u // HG - 1, par)
                    if u in work:
                        work[u]()
                if not it.here and it.before:
                    pe.wait_ge(rank_ready, 1)
                    for t in range(NT):
                        last = nc.tensor.transpose(ps_s[0][:, EARLY * t:EARLY * (t + 1)], rank[:, quarter(t)],
                                                   ident[0:EARLY, 0:EARLY])
                    last.then_inc(pos_filled, 1)

            pipeline(pe, iteration)


class Stage(Batch):

    def __init__(self, own, before=True, here=True, after=True, later=True):
        super().__init__(own, before, here, after)
        self.later = later


def program_experts(nc, io, keep, scratch, held):
    ctx = ExitStack()
    with ctx:
        def sb(name, shape, dt=F32):
            return ctx.enter_context(nc.sbuf_tensor(name, shape, dt))

        def pb(name, shape, dt=F32):
            return ctx.enter_context(nc.psum_tensor(name, shape, dt))

        def sem(name):
            held.append(nc.alloc_semaphore(name=name))
            return held[-1]

        x_all, probs_tok, pos_tok, mod, scale1, ident = (
            keep["x"], keep["probs"], keep["pos"], keep["mod"], keep["scale1"], keep["ident"])

        w1_0 = sb("w1_0", [P, E, F])
        w2_0 = sb("w2_0", [P, E, NF, D])
        w1_high = sb("w1_high", [P, E, F], F32R)
        w1_low = sb("w1_low", [P, E, F], F32R)
        w2_1 = sb("w2_1", [P, E, NF, D])
        b1 = sb("b1", [P, E, NF])
        b2 = sb("b2", [E, D])
        wq1 = sb("wq1", [P, P])
        bq1 = sb("bq1", [P, 1])
        wd = sb("wd", [P, R])
        bd = sb("bd", [R, 1])
        wu = sb("wu", [R + 1, 2 * D])
        wo1 = sb("wo1", [P, D])
        gate1 = sb("gate1", [P, E])
        shared_w = sb("shared_w", [P, D])
        shared_b = sb("shared_b", [P, D])
        slots = sb("slots", [P, KSEL])
        block_mask = sb("block_mask", [P, P + H])
        lower = sb("lower", [P, E, E])
        half = sb("half_b", [P, NT])
        acc = [sb(f"acc{i}", [P, NT, D]) for i in range(2)]
        xh_o = sb("xh_o", [P, NT, D])
        x_done = sb("x_done", [P, NT, D])
        rows = [acc[i][0:E].rearrange("p t d -> p (t d)") for i in range(2)]
        is_taken = xh_o[0:E].rearrange("p t d -> p (t d)")
        rank = x_done[0:E].rearrange("p t d -> p (t d)")
        best = sb("best_b", [E, 8])
        st_a = sb("st_a", [P, NT, 6])
        mv_a = sb("mv_a", [P, NT, 2])
        rs_a = sb("rs_a", [P, 3, NT])
        xh_a = sb("xh_a", [P, NT, D])
        xha_high = sb("xha_high", [P, NT, D], F32R)
        xha_low = sb("xha_low", [P, NT, D], F32R)
        sel = sb("sel", [P, NT, E // 2, KSEL], F32R)
        xin = sb("xin", [P, E, KSEL])
        hid0 = [sb(f"hid0_{i}", [P, NF, KSEL]) for i in range(2)]
        gsel = [sb(f"gsel{i}", [P, NT, KSEL]) for i in range(2)]
        gselT = [sb(f"gselT{i}", [P, T]) for i in range(2)]
        y0 = [sb(f"y0_{i}", [P, D]) for i in range(2)]
        gated0 = sb("gated0", [P, NT, D])
        st_b = sb("st_b", [P, NT, 6])
        mv_b = sb("mv_b", [P, NT, 2])
        rs_b = sb("rs_b", [P, 3, NT])
        xh_b = sb("xh_b", [P, NT, D])
        hT1 = sb("hT1", [P, T])
        latent = sb("latent", [R + 1, T])
        q_pos = sb("q_pos", [P, T])
        q_exp = sb("q_exp", [P, T])
        k_exp = sb("k_exp", [P, T])
        k_phi = sb("k_phi", [P, NT, D])
        v1 = sb("v1", [P, NT, D + 1])
        context = sb("context", [P, P + H])
        den = sb("den", [P, NT * H])
        den_inv = sb("den_inv", [P, NT * H])
        att1 = sb("att1", [P, NT, D])
        attT1 = sb("attT1", [P, T])
        wo1_gated = sb("wo1_gated", [P, D])
        st_f = sb("st_f", [P, NT, 6])
        mv_f = sb("mv_f", [P, NT, 2])
        rs_f = sb("rs_f", [P, 3, NT])
        xh_f = sb("xh_f", [P, NT, D])
        hT_f = sb("hT_f", [P, T])
        hTf_high = [sb(f"hTf_high{i}", [P, T], F32R) for i in range(2)]
        hTf_low = [sb(f"hTf_low{i}", [P, T], F32R) for i in range(2)]
        lmax = sb("lmax", [P, NT])
        lshift = sb("lshift", [P, NT, E])
        lexp = sb("lexp", [P, NT, E])
        lsum = sb("lsum", [P, NT])
        linv = sb("linv", [P, NT])
        prob = sb("prob", [P, NT, E])
        above = sb("above", [P, NT, E, E])
        tied = sb("tied", [P, NT, E, E])
        ahead = sb("ahead", [P, NT, E])
        top2 = sb("top2", [P, NT, E])
        tsum = sb("tsum", [P, NT])
        tinv = sb("tinv", [P, NT])
        comb = [sb(f"comb{i}", [P, NT, E]) for i in range(2)]
        combT = sb("combT", [E, T])
        sh = sb("sh", [P, NT, D])
        hid1 = [sb(f"hid1_{i}", [P, NF, T]) for i in range(2)]
        gate0 = sb("gate0", [P, D])
        gate_att1 = sb("gate_att1", [P, 2, D])
        gate_end = sb("gate_end", [P, 2, D])
        st_o = sb("st_o", [P, NT, 6])
        mv_o = sb("mv_o", [P, NT, 2])
        rs_o = sb("rs_o", [P, 3, NT])

        ps_z = [pb(f"ps_z{i}", [P, T]) for i in range(2)]
        ps_o = pb("ps_o", [P, T])
        a0 = pb("a0", [P, T])
        a1 = pb("a1", [P, T])
        a2 = pb("a2", [P, T])
        b0_ = pb("b0_", [P, T])
        b1_ = pb("b1_", [P, T])

        probs_in, slots_in, small_in, w1_0_in, w2_0_in, w1_in, w2_in, consts = (
            sem(n) for n in "probs_in slots_in small_in w1_0_in w2_0_in w1_in w2_in consts_b".split())
        w1_step, w1_ready, gate0_in, gate_att1_in, gate_end_in = (
            sem(n) for n in "w1_step w1_ready gate0_in gate_att1_in gate_end_in".split())
        xha_rounded, xha_split, hTf_rounded, hTf_split = (
            sem(n) for n in "xha_rounded xha_split hTf_rounded hTf_split".split())
        best_found, best_taken, rank_step, rank_ready, pos_filled, pos_ready = (
            sem(n) for n in "bestb_found bestb_taken rankb_step rankb_ready posb_filled posb_ready".split())
        sta_done, mva_done, ra_step, xha_ready, sel_ready = (
            sem(n) for n in "sta_done mva_done ra_step xha_ready sel_ready".split())
        g_filled, xin_ready, z0_filled, hid0_ready, gsel_ready, t_filled, gselT_ready, y0_filled, y0_ready = (
            sem(n) for n in "g_filled xin_ready z0_filled hid0_ready gsel_ready tb_filled gselT_ready "
            "y0_filled y0_ready".split())
        sc_filled, gated0_ready, x0_ready = (sem(n) for n in "sc_filled gated0_ready x0_ready".split())
        stb_done, mvb_done, rb_step, xhb_ready, hT1_filled, hT1_ready = (
            sem(n) for n in "stb_done mvb_done rb_step xhb_ready hT1_filled hT1_ready".split())
        lat_filled, lat_ready, q1_filled, qpos_ready, qmin_ready, qexp_ready, qphi_ready = (
            sem(n) for n in "lat_filled lat_ready qb_filled qpos_ready qmin_ready qexp_ready qphi_ready".split())
        uk_filled, kmin_ready, kexp_ready, kphi_ready, uv_filled, v1_ready = (
            sem(n) for n in "uk_filled kmin_ready kexp_ready kphi_ready uv_filled v1_ready".split())
        ctx_filled, ctx_ready, num_filled, den_step, den_ready, att1_ready, attT1_filled, attT1_ready = (
            sem(n) for n in "ctx_filled ctx_ready num_filled den_step den_ready att1_ready attT1_filled "
            "attT1_ready".split())
        wo1g_ready, xb1_ready, o1_filled, x1_ready = (sem(n) for n in "wo1g_ready xb1_ready o1_filled x1_ready".split())
        stf_done, mvf_done, rf_step, xhf_ready, hTf_filled, hTf_ready = (
            sem(n) for n in "stf_done mvf_done rf_step xhf_ready hTf_filled hTf_ready".split())
        l_sum, l_inv = sem("l_sum"), sem("l_inv")
        l_filled, l_step, lshift_ready, lexp_ready, top_step, comb_ready, combT_filled, combT_ready = (
            sem(n) for n in "l_filled l_step lshift_ready lexp_ready top_step comb_ready combT_filled "
            "combT_ready".split())
        sh_filled, sh_ready, shg_ready, b2_filled, acc_ready = (
            sem(n) for n in "sh_filled sh_ready shg_ready b2_filled acc_ready".split())
        z_filled, hid1_ready, o_filled, o_added = (sem(n) for n in "z_filled hid1_ready ob_filled o_added".split())
        sto_done, mvo_done, ro_step, xho_ready, outg_ready, xb2_ready, out_ready, stored = (
            sem(n) for n in "sto_done mvo_done ro_step xho_ready outg_ready xb2_ready out_ready stored".split())

        Q = 4 * E
        SMALL = 16 * 13
        block = ctx.enter_context(nc.Block())

        def pipeline(eng, iteration):
            iteration(Stage(-2, False, False, False), 0)
            iteration(Stage(-1, False, False), 1)
            iteration(Stage(0, False), 0)
            iteration(Stage(1), 1)
            with eng.Fori(0, (B - 4) // 2) as i:
                iteration(Stage(2 * i + 2), 0)
                iteration(Stage(2 * i + 3), 1)
            iteration(Stage(B - 2, later=False), B % 2)
            iteration(Stage(B - 1, after=False, later=False), (B - 1) % 2)
            iteration(Stage(B, here=False, after=False, later=False), B % 2)

        def tokens(ap):
            return ap.rearrange("p (t n) -> p t n", t=NT)

        def quarter(t):
            return slice(P * t, P * (t + 1))

        def over_tokens(ap):
            return ap.unsqueeze(1).to_broadcast([P, NT, D])

        @block.sync
        def _(sp):
            sp.dma_start(slots[:], io["slots"].partition_broadcast(P)).then_inc(slots_in, 16)
            sp.dma_start(rows[0], scratch["probs"].ap()[B - 1]).then_inc(probs_in, 16)
            sp.dma_start(w1_0[:], io["w1_0"].rearrange("e d f -> d e f")).then_inc(w1_0_in, 16)
            sp.dma_start(w2_0[:], io["w2_0"].rearrange("e (n p) d -> p e n d", p=P)).then_inc(w2_0_in, 16)
            for tile, name in ((shared_b, "shared_b"), (lower, "lower")):
                sp.dma_start(tile[:], io[name].partition_broadcast(P)).then_inc(small_in, 16)
            for tile, name in ((block_mask, "block_mask"), (b1, "b1"), (b2, "b2"), (wq1, "wq1"), (bq1, "bq1"),
                               (wd, "wd"), (bd, "bd"), (wu, "wu"), (wo1, "wo1"), (gate1, "gate1"),
                               (shared_w, "shared_w")):
                sp.dma_start(tile[:], io[name]).then_inc(small_in, 16)
            for i in range(2):
                sp.dma_start(hid1[i][:], io["w1_1"][E // 2 * i:E // 2 * (i + 1)].rearrange("e d f -> d e f")
                             ).then_inc(w1_in, 16)
            sp.dma_start(w2_1[:], io["w2_1"].rearrange("e (n p) d -> p e n d", p=P)).then_inc(w2_in, 16)

            def gate_rows(tile, k, n, bb, loaded):
                sp.dma_start(tile, scratch["gates"].ap()[k:k + n, bass.ds(bb, 1), :].partition_broadcast(P)
                             ).then_inc(loaded, 16)

            gate_rows(gate_att1[:], 3, 2, 0, gate_att1_in)

            def iteration(it, par):
                nxt, nn, prev = it.own + 1, it.own + 2, it.own - 1
                if it.before:
                    sp.wait_ge(xb2_ready, prev)
                    sp.wait_ge(outg_ready, prev)
                    settle(sp)
                    gate_rows(gate_end[:], 5, 2, prev, gate_end_in)
                if it.later:
                    sp.wait_ge(gated0_ready, nn)
                    settle(sp)
                    gate_rows(gate0[:], 2, 1, nn, gate0_in)
                if it.after and it.later:
                    sp.wait_ge(xb1_ready, nxt + 1)
                    sp.wait_ge(wo1g_ready, nxt + 1)
                    settle(sp)
                    gate_rows(gate_att1[:], 3, 2, nxt + 1, gate_att1_in)
                if it.before:
                    sp.wait_ge(out_ready, prev + 1)
                    sp.dma_start(io["out"][prev].rearrange("(t p) d -> p t d", p=P), x_done[:]).then_inc(stored, 16)

            pipeline(sp, iteration)
            sp.wait_ge(stored, 16 * B)

        @block.gpsimd
        def _(pool):
            nc.gpsimd.memset(half[:], -0.5).then_inc(consts, 1)
            pool.wait_ge(consts, 1)
            nc.gpsimd.memset(latent[R:R + 1, :], 1.0).then_inc(consts, 1)
            pool.wait_ge(consts, 2)
            nc.gpsimd.memset(v1[:, :, D:D + 1], 1.0).then_inc(consts, 1)
            pool.wait_ge(consts, 3)

            def add_vector(bb, row, ready):
                settle(pool)
                for t in range(NT):
                    last = nc.gpsimd.tensor_tensor(x_all[:, bb, t, :], x_all[:, bb, t, :], row, ALU.add)
                last.then_inc(ready, 1)

            def norm_a(m):
                pool.wait_ge(mva_done, m + 1)
                pool.wait_ge(xha_split, m)
                norm(nc, half, x_all[:, m], mv_a, rs_a, ra_step, m, xh_a, xha_ready)

            def split_w1():
                pool.wait_ge(w1_in, 32)
                for i in range(2):
                    half_of = slice(E // 2 * i, E // 2 * (i + 1))
                    nc.gpsimd.tensor_copy(w1_high[:, half_of], hid1[i][:]).then_inc(w1_step, 1)
                    pool.wait_ge(w1_step, i + 1)
                    nc.gpsimd.tensor_tensor(w1_low[:, half_of], hid1[i][:], w1_high[:, half_of], ALU.subtract
                                            ).then_inc(w1_ready, 1)

            def iteration(it, par):
                b, nxt, nn, prev = it.own, it.own + 1, it.own + 2, it.own - 1
                if it.later and (it.here or not it.after):
                    norm_a(nn)
                if it.after:
                    pool.wait_ge(mvb_done, nxt + 1)
                    pool.wait_ge(hT1_filled, nxt)
                    norm(nc, half, x_all[:, nxt], mv_b, rs_b, rb_step, nxt, xh_b, xhb_ready)
                elif it.later:
                    norm_a(1)
                    split_w1()
                if it.after:
                    pool.wait_ge(xhb_ready, nxt + 1)
                    pool.wait_ge(gate_att1_in, 16 * (nxt + 1))
                    add_vector(nxt, gate_att1[:, 1, :], xb1_ready)
                    pool.wait_ge(o1_filled, nxt)
                    pool.wait_ge(small_in, SMALL)
                    nc.gpsimd.tensor_tensor(wo1_gated[:], wo1[:], gate_att1[:, 0, :], ALU.mult).then_inc(wo1g_ready, 1)
                if it.before:
                    pool.wait_ge(gate_end_in, 16 * (prev + 1))
                    add_vector(prev, gate_end[:, 1, :], xb2_ready)
                    pool.wait_ge(mvo_done, prev + 1)
                    pool.wait_ge(out_ready, prev)
                    norm(nc, half, acc[1 - par][:], mv_o, rs_o, ro_step, prev, xh_o, xho_ready)
                if it.after:
                    pool.wait_ge(qexp_ready, nxt + 1)
                    pool.wait_ge(qpos_ready, nxt + 1)
                    nc.gpsimd.tensor_tensor(q_exp[:], q_exp[:], q_pos[:], ALU.add).then_inc(qphi_ready, 1)
                    pool.wait_ge(mvf_done, nxt + 1)
                    pool.wait_ge(hTf_filled, nxt)
                    norm(nc, half, x_all[:, nxt], mv_f, rs_f, rf_step, nxt, xh_f, xhf_ready)
                if it.later:
                    pool.wait_ge(gated0_ready, nn + 1)
                    settle(pool)
                    nc.gpsimd.tensor_tensor(x_all[:, nn], x_all[:, nn], gated0[:], ALU.add).then_inc(x0_ready, 1)

            pipeline(pool, iteration)

        @block.scalar
        def _(act):
            def gelu_quarter(b, q, par):
                e, n = q // 4, q % 4
                act.wait_ge(z_filled, Q * b + q + 1)
                if n == 0 and (e or not (isinstance(b, int) and b == 0)):
                    act.wait_ge(o_filled, E * b + e - 1)
                nc.scalar.activation(hid1[e % 2][:, n, :], ps_z[q % 2][:], ACT.Gelu, bias=b1[:, e, n:n + 1]
                                     ).then_inc(hid1_ready, 1)

            def iteration(it, par):
                b, nxt, nn, prev = it.own, it.own + 1, it.own + 2, it.own - 1

                def gathered(g):
                    act.wait_ge(g_filled, 2 * nn + g + 1)
                    act.wait_ge(z0_filled, E * nn)
                    settle(act)
                    nc.scalar.activation(xin[:, 4 * g:4 * g + 4, :].rearrange("p e k -> p (e k)"), (a0, a1)[g][:],
                                         ACT.Identity, scale=scale1[:, 0, 1, bass.ds(nn, 1)],
                                         bias=mod[:, 0, SHIFT_B, bass.ds(nn, 1)]).then_inc(xin_ready, 1)

                def gelu0(e):
                    act.wait_ge(z0_filled, E * nn + e + 1)
                    if e >= 2 or not (isinstance(nn, int) and nn == 0):
                        act.wait_ge(y0_filled, E * nn + e - 1)
                    nc.scalar.activation(hid0[e % 2][:].rearrange("p n k -> p (n k)"), a0[:], ACT.Gelu
                                         ).then_inc(hid0_ready, 1)

                def save_gselT(e):
                    bank = a1 if it.here else ps_z[0]
                    act.wait_ge(t_filled, E * nn + e + 1)
                    if e >= 2 or not (isinstance(nn, int) and nn == 0):
                        act.wait_ge(sc_filled, E * nn + e - 1)
                    nc.scalar.copy(gselT[e % 2][:], bank[:]).then_inc(gselT_ready, 1)

                def shift_1():
                    act.wait_ge(hT1_filled, nxt + 1)
                    act.wait_ge(q1_filled, nxt)
                    nc.scalar.activation(hT1[:], b0_[:], ACT.Identity, scale=scale1[:, 1, 0, bass.ds(nxt, 1)],
                                         bias=mod[:, 1, SHIFT_A, bass.ds(nxt, 1)]).then_inc(hT1_ready, 1)

                def save_latent():
                    act.wait_ge(lat_filled, nxt + 1)
                    act.wait_ge(uv_filled, nxt)
                    act.wait_ge(small_in, SMALL)
                    nc.scalar.activation(latent[0:R, :], b1_[0:R, :], ACT.Identity, bias=bd[:]).then_inc(lat_ready, 1)

                def q_positive():
                    act.wait_ge(q1_filled, nxt + 1)
                    act.wait_ge(qphi_ready, nxt)
                    nc.scalar.activation(q_pos[:], b0_[:], ACT.Relu, bias=bq1[:]).then_inc(qpos_ready, 1)

                def exp_qk():
                    act.wait_ge(qmin_ready, nxt + 1)
                    nc.scalar.activation(q_exp[:], q_exp[:], ACT.Exp).then_inc(qexp_ready, 1)
                    act.wait_ge(kmin_ready, nxt + 1)
                    nc.scalar.activation(k_exp[:], k_exp[:], ACT.Exp).then_inc(kexp_ready, 1)

                def save_v1():
                    act.wait_ge(uv_filled, nxt + 1)
                    act.wait_ge(ctx_filled, nxt)
                    nc.scalar.copy(v1[:, :, 0:D], tokens(b0_[:])).then_inc(v1_ready, 1)

                def save_attT1():
                    act.wait_ge(attT1_filled, nxt + 1)
                    act.wait_ge(o1_filled, nxt)
                    nc.scalar.copy(attT1[:], b0_[:]).then_inc(attT1_ready, 1)

                def shift_f():
                    act.wait_ge(hTf_filled, nxt + 1)
                    act.wait_ge(sh_filled, nxt)
                    act.wait_ge(hTf_split, nxt)
                    nc.scalar.activation(hT_f[:], b0_[:], ACT.Identity, scale=scale1[:, 1, 1, bass.ds(nxt, 1)],
                                         bias=mod[:, 1, SHIFT_B, bass.ds(nxt, 1)]).then_inc(hTf_ready, 1)
                    act.wait_ge(hTf_ready, nxt + 1)
                    if it.before:
                        act.wait_ge(z_filled, Q * b)
                    nc.scalar.copy(hTf_high[1 - par][:], hT_f[:]).then_inc(hTf_rounded, 1)

                def exp_router():
                    act.wait_ge(lshift_ready, nxt + 1)
                    act.wait_ge(comb_ready, nxt)
                    nc.scalar.activation(lexp[:], lshift[:], ACT.Exp).then_inc(lexp_ready, 1)

                def gelu_shared():
                    act.wait_ge(sh_ready, nxt + 1)
                    nc.scalar.activation(sh[:], sh[:], ACT.Gelu).then_inc(shg_ready, 1)

                def save_combT():
                    act.wait_ge(combT_filled, nxt + 1)
                    act.wait_ge(b2_filled, nxt)
                    nc.scalar.copy(combT[:], b1_[0:E, :]).then_inc(combT_ready, 1)

                work = {q: [] for q in range(Q)}
                if it.after:
                    for q, f in ((6, shift_1), (8, save_latent), (9, q_positive), (11, exp_qk), (12, save_v1),
                                 (20, save_attT1), (26, shift_f), (28, exp_router), (29, gelu_shared),
                                 (30, save_combT)):
                        work[q].append(f)
                if it.later:
                    work[4].append(lambda: gathered(0))
                    work[6].append(lambda: gathered(1))
                    for e in range(E):
                        if it.here:
                            work[6 + 3 * e].append(lambda e=e: save_gselT(e))
                            work[7 + 3 * e].append(lambda e=e: gelu0(e))
                        else:
                            work[6 + 3 * e] += [lambda e=e: gelu0(e), lambda e=e: save_gselT(e)]
                for q in range(Q):
                    if it.here:
                        gelu_quarter(b, q, par)
                    for f in work[q]:
                        f()

            pipeline(act, iteration)

        @block.vector
        def _(dve):
            def statistics(xin_, st, mv, st_done, mv_done, bb, read):
                dve.wait_ge(read, bb)
                settle(dve)
                for t in range(NT):
                    last = nc.vector.bn_stats(st[:, t, :], xin_[:, t, :])
                last.then_inc(st_done, 1)
                dve.wait_ge(st_done, bb + 1)
                settle(dve)
                for t in range(NT):
                    last = nc.vector.bn_aggr(mv[:, t, :], st[:, t, :])
                last.then_inc(mv_done, 1)

            statistics(x_all[:, 0], st_a, mv_a, sta_done, mva_done, 0, xha_ready)
            dve.wait_ge(slots_in, 16)

            def iteration(it, par):
                b, nxt, nn, prev = it.own, it.own + 1, it.own + 2, it.own - 1

                def add_expert(bb, e, pp):
                    dve.wait_ge(o_filled, E * bb + e + 1)
                    if e == 0:
                        dve.wait_ge(acc_ready, bb + 1)
                    dve.wait_ge(o_added, E * bb + e)
                    for t in range(NT):
                        last = nc.vector.scalar_tensor_tensor(acc[pp][:, t, :], ps_o[:, quarter(t)],
                                                              comb[pp][:, t, e:e + 1], acc[pp][:, t, :],
                                                              ALU.mult, ALU.add)
                    last.then_inc(o_added, 1)

                def finish_stats():
                    dve.wait_ge(o_added, E * b)
                    statistics(acc[1 - par], st_o, mv_o, sto_done, mvo_done, prev, xho_ready)

                def finish():
                    dve.wait_ge(xho_ready, prev + 1)
                    dve.wait_ge(gate_end_in, 16 * (prev + 1))
                    nc.vector.tensor_tensor(xh_o[:], xh_o[:], over_tokens(gate_end[:, 0, :]), ALU.mult
                                            ).then_inc(outg_ready, 1)
                    dve.wait_ge(outg_ready, prev + 1)
                    dve.wait_ge(xb2_ready, prev + 1)
                    dve.wait_ge(stored, 16 * prev)
                    nc.vector.tensor_tensor(x_done[:], xh_o[:], x_all[:, prev], ALU.add).then_inc(out_ready, 1)

                def start_b():
                    dve.wait_ge(x0_ready, nxt + 1)
                    statistics(x_all[:, nxt], st_b, mv_b, stb_done, mvb_done, nxt, xhb_ready)

                def select(m, g):
                    dve.wait_ge(g_filled, 2 * m + g)
                    for t in range(NT):
                        last = nc.vector.tensor_tensor(
                            sel[:, t], slots[:].unsqueeze(1).to_broadcast([P, E // 2, KSEL]),
                            pos_tok[:, m, t, 4 * g:4 * g + 4].unsqueeze(2).to_broadcast([P, E // 2, KSEL]),
                            ALU.is_equal)
                    last.then_inc(sel_ready, 1)

                def start_a(m):
                    statistics(x_all[:, m], st_a, mv_a, sta_done, mva_done, m, xha_ready)


                def split_a(m):
                    dve.wait_ge(xha_ready, m + 1)
                    dve.wait_ge(g_filled, 2 * m)
                    nc.vector.tensor_copy(xha_high[:], xh_a[:]).then_inc(xha_rounded, 1)
                    dve.wait_ge(xha_rounded, m + 1)
                    nc.vector.tensor_tensor(xha_low[:], xh_a[:], xha_high[:], ALU.subtract).then_inc(xha_split, 1)

                def split_f():
                    dve.wait_ge(hTf_rounded, nxt + 1)
                    nc.vector.tensor_tensor(hTf_low[1 - par][:], hT_f[:], hTf_high[1 - par][:], ALU.subtract
                                            ).then_inc(hTf_split, 1)

                def select_gated(e):
                    if e >= 2 or not (isinstance(nn, int) and nn == 0):
                        dve.wait_ge(t_filled, E * nn + e - 1)
                    for t in range(NT):
                        last = nc.vector.tensor_scalar(gsel[e % 2][:, t, :], slots[:], pos_tok[:, nn, t, e:e + 1],
                                                       probs_tok[:, nn, t, e:e + 1], ALU.is_equal, ALU.mult)
                    last.then_inc(gsel_ready, 1)

                def save_y0(e):
                    dve.wait_ge(y0_filled, E * nn + e + 1)
                    if e >= 2 or not (isinstance(nn, int) and nn == 0):
                        dve.wait_ge(sc_filled, E * nn + e - 1)
                    nc.vector.tensor_copy(y0[e % 2][:], a1[:, 0:D]).then_inc(y0_ready, 1)

                def gate_0():
                    dve.wait_ge(sc_filled, E * (nn + 1))
                    dve.wait_ge(x0_ready, nn)
                    dve.wait_ge(gate0_in, 16 * (nn + 1))
                    nc.vector.tensor_tensor(gated0[:], tokens(a2[:]), over_tokens(gate0[:]), ALU.mult
                                            ).then_inc(gated0_ready, 1)

                def take_last(n):
                    if n == 0:
                        dve.wait_ge(probs_in, 16)
                    take_best(nc, rows, best[:], best_found, best_taken, n)

                def place_last():
                    dve.wait_ge(pos_filled, 1)
                    nc.vector.tensor_copy(pos_tok[:, B - 1], ps_o[:, 0:NT * E].rearrange("p (t e) -> p t e", t=NT)
                                          ).then_inc(pos_ready, 1)

                def q_negative():
                    if not it.here:
                        dve.wait_ge(small_in, SMALL)
                    dve.wait_ge(qpos_ready, nxt + 1)
                    dve.wait_ge(num_filled, nxt)
                    nc.vector.tensor_scalar(q_exp[:], b0_[:], bq1[:], 0.0, ALU.add, ALU.min).then_inc(qmin_ready, 1)

                def k_negative():
                    dve.wait_ge(uk_filled, nxt + 1)
                    dve.wait_ge(kphi_ready, nxt)
                    nc.vector.tensor_scalar(k_exp[:], b1_[:], 0.0, None, ALU.min).then_inc(kmin_ready, 1)

                def k_features():
                    dve.wait_ge(kexp_ready, nxt + 1)
                    dve.wait_ge(ctx_filled, nxt)
                    nc.vector.scalar_tensor_tensor(k_phi[:].rearrange("p t n -> p (t n)"), b1_[:], 0.0, k_exp[:],
                                                   ALU.max, ALU.add).then_inc(kphi_ready, 1)

                def mask_context():
                    dve.wait_ge(ctx_filled, nxt + 1)
                    dve.wait_ge(num_filled, nxt)
                    nc.vector.tensor_tensor(context[:, 0:P], b1_[:, 0:P], block_mask[:, 0:P], ALU.mult)
                    nc.vector.tensor_scalar(context[:, P:P + H], block_mask[:, P:P + H], b1_[:, P:P + 1], None,
                                            ALU.mult).then_inc(ctx_ready, 1)

                def divide():
                    dve.wait_ge(num_filled, nxt + 1)
                    nc.vector.tensor_scalar(den[:], b1_[:, 0:NT * H], 1e-6, None, ALU.add).then_inc(den_step, 1)
                    dve.wait_ge(den_step, nxt + 1)
                    dve.wait_ge(att1_ready, nxt)
                    nc.vector.reciprocal(den_inv[:], den[:]).then_inc(den_ready, 1)
                    dve.wait_ge(den_ready, nxt + 1)
                    dve.wait_ge(attT1_filled, nxt)
                    nc.vector.tensor_tensor(att1[:].rearrange("p t (h e) -> p (t h) e", e=HD),
                                            b0_[:].rearrange("p (n e) -> p n e", e=HD),
                                            den_inv[:].unsqueeze(2).to_broadcast([P, NT * H, HD]), ALU.mult
                                            ).then_inc(att1_ready, 1)

                def residual_1():
                    dve.wait_ge(o1_filled, nxt + 1)
                    dve.wait_ge(xb1_ready, nxt + 1)
                    nc.vector.tensor_tensor(x_all[:, nxt], tokens(b1_[:]), x_all[:, nxt], ALU.add).then_inc(x1_ready, 1)
                    dve.wait_ge(x1_ready, nxt + 1)
                    statistics(x_all[:, nxt], st_f, mv_f, stf_done, mvf_done, nxt, xhf_ready)

                def shift_logits():
                    dve.wait_ge(l_filled, nxt + 1)
                    v = b1_[:, 0:NT * E].rearrange("p (t e) -> p t e", t=NT)
                    nc.vector.tensor_reduce(lmax[:], v, AX.X, ALU.max).then_inc(l_step, 1)
                    dve.wait_ge(l_step, nxt + 1)
                    dve.wait_ge(lexp_ready, nxt)
                    nc.vector.tensor_tensor(lshift[:], v, lmax[:].unsqueeze(2).to_broadcast([P, NT, E]), ALU.subtract
                                            ).then_inc(lshift_ready, 1)

                def best_two():
                    done = 9 * nxt

                    def step(n, ins):
                        ins.then_inc(top_step, 1)
                        dve.wait_ge(top_step, done + n)

                    def of(ap, axis):
                        return ap.unsqueeze(axis).to_broadcast([P, NT, E, E])

                    dve.wait_ge(lexp_ready, nxt + 1)
                    step(1, nc.vector.tensor_reduce(lsum[:], lexp[:], AX.X, ALU.add))
                    step(2, nc.vector.reciprocal(linv[:], lsum[:]))
                    step(3, nc.vector.tensor_tensor(prob[:], lexp[:], linv[:].unsqueeze(2).to_broadcast([P, NT, E]),
                                                    ALU.mult))
                    nc.vector.tensor_tensor(above[:], of(prob[:], 2), of(prob[:], 3), ALU.is_gt).then_inc(top_step, 1)
                    step(5, nc.vector.tensor_tensor(tied[:], of(prob[:], 2), of(prob[:], 3), ALU.is_equal))
                    step(6, nc.vector.tensor_tensor(tied[:], tied[:], lower[:].unsqueeze(1).to_broadcast([P, NT, E, E]),
                                                    ALU.mult))
                    step(7, nc.vector.tensor_tensor(above[:], above[:], tied[:], ALU.add))
                    step(8, nc.vector.tensor_reduce(ahead[:], above[:], AX.X, ALU.add))
                    step(9, nc.vector.scalar_tensor_tensor(top2[:], ahead[:], 1.5, prob[:], ALU.is_lt, ALU.mult))

                def combine():
                    nc.vector.tensor_reduce(tsum[:], top2[:], AX.X, ALU.add).then_inc(l_sum, 1)
                    dve.wait_ge(l_sum, nxt + 1)
                    nc.vector.reciprocal(tinv[:], tsum[:]).then_inc(l_inv, 1)
                    dve.wait_ge(l_inv, nxt + 1)
                    nc.vector.tensor_tensor(comb[1 - par][:], top2[:], tinv[:].unsqueeze(2).to_broadcast([P, NT, E]),
                                            ALU.mult).then_inc(comb_ready, 1)

                def shared():
                    dve.wait_ge(sh_filled, nxt + 1)
                    dve.wait_ge(acc_ready, nxt)
                    nc.vector.tensor_tensor(sh[:], tokens(b0_[:]), over_tokens(shared_b[:]), ALU.add
                                            ).then_inc(sh_ready, 1)

                def start_acc():
                    dve.wait_ge(shg_ready, b + 1)
                    dve.wait_ge(b2_filled, b + 1)
                    if it.before:
                        dve.wait_ge(xho_ready, b - 1)
                    nc.vector.scalar_tensor_tensor(acc[par][:], sh[:], 0.5, tokens(b0_[:]), ALU.mult, ALU.add
                                                   ).then_inc(acc_ready, 1)

                work = {q: [] for q in range(Q)}
                if it.before:
                    work[6].append(finish_stats)
                    work[11].append(finish)
                if it.here and it.later:
                    work[0] += [lambda: start_a(nn), lambda: select(nn, 0)]
                    work[1].append(lambda: split_a(nn))
                elif it.later and not it.after:
                    work[0].append(lambda: select(0, 0))
                    work[1].append(lambda: split_a(0))
                    work[2].append(lambda: start_a(1))
                    work[30] += [lambda: select(1, 0), lambda: split_a(1)]
                if it.after:
                    for q, f in ((0, start_b), (10, q_negative), (10, k_negative), (12, k_features), (15, mask_context),
                                 (17, divide), (22, residual_1), (27, shift_logits), (28, split_f), (29, best_two),
                                 (29, combine),
                                 (28, shared)):
                        work[q].append(f)
                if it.here:
                    work[4].append(start_acc)
                elif it.later:
                    for n in range(ROUNDS // 2):
                        work[6 + 3 * n].append(lambda n=n: take_last(ROUNDS // 2 * (b + 2) + n))
                    if it.after:
                        work[28].append(lambda: rank_taken(nc, rows, is_taken, rank, best_taken, rank_step, rank_ready))
                        work[31].append(place_last)
                if it.later:
                    work[4].append(lambda: select(nn, 1))
                    work[5] += [lambda: select_gated(0), lambda: select_gated(1)]
                    for e in range(E):
                        q = (8 if it.here else 7) + 3 * e
                        work[q].append(lambda e=e: save_y0(e))
                        if e + 2 < E:
                            work[q].append(lambda e=e: select_gated(e + 2))
                    work[31].append(gate_0)
                for q in range(Q):
                    if q == 3 and it.before:
                        add_expert(prev, E - 1, 1 - par)
                    elif q % 4 == 3 and q > 3 and it.here:
                        add_expert(b, q // 4 - 1, par)
                    for f in work[q]:
                        f()

            pipeline(dve, iteration)

        @block.tensor
        def _(pe):
            def hidden_quarter(b, q, par):
                e, n = q // 4, q % 4
                if q == 0:
                    pe.wait_ge(hTf_split, b + 1)
                    pe.wait_ge(gselT_ready, 2 * E)
                    pe.wait_ge(pos_ready, 1)
                    pe.wait_ge(w1_ready, 2)
                if q >= 2 or not (isinstance(b, int) and b == 0):
                    pe.wait_ge(hid1_ready, Q * b + q - 1)
                nc.tensor.matmul(ps_z[q % 2][:], w1_high[:, e, quarter(n)], hTf_high[par][:], start=True, stop=False)
                nc.tensor.matmul(ps_z[q % 2][:], w1_high[:, e, quarter(n)], hTf_low[par][:], start=False, stop=False)
                nc.tensor.matmul(ps_z[q % 2][:], w1_low[:, e, quarter(n)], hTf_high[par][:], start=False, stop=True
                                 ).then_inc(z_filled, 1)

            def outputs(b, e, step):
                if step == 0:
                    pe.wait_ge(w2_in, 16)
                    pe.wait_ge(hid1_ready, Q * b + 4 * (e + 1))
                    pe.wait_ge(o_added, E * b + e)
                for t in ((0,), (1, 2), (3,), ())[step]:
                    for f in range(NF):
                        last = nc.tensor.matmul(ps_o[:, quarter(t)], hid1[e % 2][:, f, quarter(t)], w2_1[:, e, f, :],
                                                start=(f == 0), stop=(f == NF - 1))
                if step == 2:
                    last.then_inc(o_filled, 1)

            def transposes(bank, of, filled):
                for t in range(NT):
                    last = nc.tensor.transpose(bank[:, quarter(t)], of(t), ident[:])
                last.then_inc(filled, 1)

            def by_token(bank, lhs, rhs, width, filled):
                for t in range(NT):
                    last = nc.tensor.matmul(bank[:, width * t:width * (t + 1)], lhs(t), rhs, start=True, stop=True)
                last.then_inc(filled, 1)

            def iteration(it, par):
                b, nxt, nn, prev = it.own, it.own + 1, it.own + 2, it.own - 1

                def gather(g):
                    if g == 0:
                        pe.wait_ge(hid0_ready, E * nn)
                        pe.wait_ge(xha_split, nn + 1)
                    else:
                        pe.wait_ge(y0_ready, E * nn)
                    pe.wait_ge(sel_ready, 2 * nn + g + 1)
                    for t in range(NT):
                        for part in (xha_high, xha_low):
                            last = nc.tensor.matmul((a0, a1)[g][:], part[:, t, :],
                                                    sel[:, t].rearrange("p e k -> p (e k)"),
                                                    start=(t == 0 and part is xha_high),
                                                    stop=(t == NT - 1 and part is xha_low))
                    last.then_inc(g_filled, 1)

                def gated_T(e):
                    bank = a1 if it.here else ps_z[0]
                    pe.wait_ge(gsel_ready, E * nn + e + 1)
                    if not it.here:
                        pe.wait_ge(gselT_ready, E * nn + e)
                    elif e == 0:
                        pe.wait_ge(xin_ready, 2 * nn + 2)
                    else:
                        pe.wait_ge(y0_ready, E * nn + e)
                    transposes(bank, lambda t: gsel[e % 2][:, t, :], t_filled)

                def hidden0(e):
                    pe.wait_ge(w1_0_in, 16)
                    pe.wait_ge(xin_ready, 2 * nn + 1 + e // 4)
                    pe.wait_ge(hid0_ready, E * nn + e)
                    for f in range(NF):
                        last = nc.tensor.matmul(a0[:, quarter(f)], w1_0[:, e, quarter(f)], xin[:, e, :],
                                                start=True, stop=True)
                    last.then_inc(z0_filled, 1)

                def output0(e):
                    pe.wait_ge(w2_0_in, 16)
                    pe.wait_ge(hid0_ready, E * nn + e + 1)
                    if it.here:
                        pe.wait_ge(gselT_ready, E * nn + e + 1)
                    elif e == 0:
                        pe.wait_ge(xin_ready, 2 * nn + 2)
                    else:
                        pe.wait_ge(y0_ready, E * nn + e)
                    for f in range(NF):
                        last = nc.tensor.matmul(a1[:, 0:D], hid0[e % 2][:, f, :], w2_0[:, e, f, :],
                                                start=(f == 0), stop=(f == NF - 1))
                    last.then_inc(y0_filled, 1)

                def scatter(e):
                    pe.wait_ge(y0_ready, E * nn + e + 1)
                    pe.wait_ge(gselT_ready, E * nn + e + 1)
                    if e == 0:
                        pe.wait_ge(gated0_ready, nn)
                    for t in range(NT):
                        last = nc.tensor.matmul(a2[:, quarter(t)], gselT[e % 2][:, quarter(t)], y0[e % 2][:],
                                                start=(e == 0 and t == 0), stop=(e == E - 1), skip_group_check=True)
                    last.then_inc(sc_filled, 1)

                def place_last():
                    pe.wait_ge(rank_ready, 1)
                    for t in range(NT):
                        last = nc.tensor.transpose(ps_o[:, E * t:E * (t + 1)], rank[:, quarter(t)], ident[0:E, 0:E])
                    last.then_inc(pos_filled, 1)

                def norm1_T():
                    if not it.here:
                        pe.wait_ge(small_in, SMALL)
                    pe.wait_ge(xhb_ready, nxt + 1)
                    pe.wait_ge(acc_ready, nxt)
                    transposes(b0_, lambda t: xh_b[:, t, :], hT1_filled)

                def latents():
                    pe.wait_ge(hT1_ready, nxt + 1)
                    pe.wait_ge(combT_ready, nxt)
                    nc.tensor.matmul(b1_[0:R, :], wd[:], hT1[:], start=True, stop=True).then_inc(lat_filled, 1)

                def queries():
                    nc.tensor.matmul(b0_[:], wq1[:], hT1[:], start=True, stop=True).then_inc(q1_filled, 1)

                def keys():
                    pe.wait_ge(lat_ready, nxt + 1)
                    by_token(b1_, lambda t: latent[:, quarter(t)], wu[:, 0:D], D, uk_filled)

                def values():
                    pe.wait_ge(qpos_ready, nxt + 1)
                    pe.wait_ge(qmin_ready, nxt + 1)
                    by_token(b0_, lambda t: latent[:, quarter(t)], wu[:, D:2 * D], D, uv_filled)

                def contexts():
                    pe.wait_ge(kphi_ready, nxt + 1)
                    pe.wait_ge(v1_ready, nxt + 1)
                    for t in range(NT):
                        last = nc.tensor.matmul(b1_[:, 0:D + 1], k_phi[:, t, :], v1[:, t, :],
                                                start=(t == 0), stop=(t == NT - 1))
                    last.then_inc(ctx_filled, 1)

                def attend():
                    pe.wait_ge(ctx_ready, nxt + 1)
                    pe.wait_ge(qphi_ready, nxt + 1)
                    for t in range(NT):
                        nc.tensor.matmul(b0_[:, quarter(t)], q_exp[:, quarter(t)], context[:, 0:P],
                                         start=True, stop=True)
                        last = nc.tensor.matmul(b1_[:, H * t:H * (t + 1)], q_exp[:, quarter(t)], context[:, P:P + H],
                                                start=True, stop=True)
                    last.then_inc(num_filled, 1)

                def att_T():
                    pe.wait_ge(att1_ready, nxt + 1)
                    transposes(b0_, lambda t: att1[:, t, :], attT1_filled)

                def project_o():
                    pe.wait_ge(attT1_ready, nxt + 1)
                    pe.wait_ge(wo1g_ready, nxt + 1)
                    by_token(b1_, lambda t: attT1[:, quarter(t)], wo1_gated[:], D, o1_filled)

                def norm2_T():
                    pe.wait_ge(xhf_ready, nxt + 1)
                    transposes(b0_, lambda t: xh_f[:, t, :], hTf_filled)

                def logits():
                    pe.wait_ge(hTf_ready, nxt + 1)
                    pe.wait_ge(x1_ready, nxt + 1)
                    by_token(b1_, lambda t: hT_f[:, quarter(t)], gate1[:], E, l_filled)

                def shared():
                    by_token(b0_, lambda t: hT_f[:, quarter(t)], shared_w[:], D, sh_filled)

                def comb_T():
                    pe.wait_ge(comb_ready, nxt + 1)
                    for t in range(NT):
                        last = nc.tensor.transpose(b1_[0:E, quarter(t)], comb[1 - par][:, t, :], ident[:])
                    last.then_inc(combT_filled, 1)

                def biases():
                    pe.wait_ge(combT_ready, nxt + 1)
                    pe.wait_ge(sh_ready, nxt + 1)
                    by_token(b0_, lambda t: combT[:, quarter(t)], b2[:], D, b2_filled)

                work = {q: [] for q in range(Q)}
                if it.after:
                    for q, f in ((5, norm1_T), (7, latents), (8, queries), (10, keys), (10, values), (14, contexts),
                                 (17, attend), (19, att_T), (21, project_o), (25, norm2_T), (27, logits),
                                 (28, shared), (30, comb_T), (31, biases)):
                        work[q].append(f)
                if it.after and not it.here:
                    work[30].append(place_last)
                if it.later:
                    work[3].append(lambda: gather(0))
                    work[5].append(lambda: gather(1))
                    for e in range(E):
                        if it.here:
                            work[6 + 3 * e] += [lambda e=e: gated_T(e), lambda e=e: hidden0(e)]
                            work[8 + 3 * e].append(lambda e=e: output0(e))
                            work[9 + 3 * e].append(lambda e=e: scatter(e))
                        else:
                            work[6 + 3 * e].append(lambda e=e: hidden0(e))
                            if e:
                                work[6 + 3 * e].append(lambda e=e: scatter(e - 1))
                            work[6 + 3 * e].append(lambda e=e: gated_T(e))
                            work[7 + 3 * e].append(lambda e=e: output0(e))
                    if not it.here:
                        work[6 + 3 * E].append(lambda: scatter(E - 1))
                for q in range(Q):
                    if it.here:
                        hidden_quarter(b, q, par)
                    if q < 4:
                        if it.before:
                            outputs(prev, E - 1, q)
                    elif it.here:
                        outputs(b, q // 4 - 1, q % 4)
                    for f in work[q]:
                        f()

            pipeline(pe, iteration)


def build(nc, io):
    scratch = {"k": nc.dram_tensor("k_parts_dram", (PARTS * HD, H, T), BF16, kind="Internal"),
               "q": nc.dram_tensor("q_parts_dram", (QSLOTS * HD, H, T), BF16, kind="Internal"),
               "gates": nc.dram_tensor("gates_dram", (7, B, D), F32, kind="Internal"),
               "probs": nc.dram_tensor("probs_dram", (B, E, T), F32, kind="Internal")}
    with ExitStack() as ctx:
        shapes = {"x": [P, B, NT, D], "probs": [P, B, NT, E], "pos": [P, B, NT, E], "mod": [P, 2, 6, B],
                  "scale1": [P, 2, 2, B],
                  "ident": [P, P]}
        keep = {name: ctx.enter_context(nc.sbuf_tensor(name, shape, F32)) for name, shape in shapes.items()}
        held = []
        program_attention(nc, io, keep, scratch, held)
        nc.all_engine_barrier()
        nc.clear_and_free_semaphores(held)
        nc.all_engine_barrier()
        program_experts(nc, io, keep, scratch, [])


def laid_out(v):
    import numpy as np

    eye = np.eye(P, dtype=np.float32)
    head = np.arange(P) // HD
    return {
        "x": v["L0_attn_x"],
        "cT": np.stack([v["L0_c"].T, v["L1_c"].T], 1),
        "wmod": np.stack([v["L0_wmod"], v["L1_wmod"]], 1),
        "ident": eye,
        "wq": v["L0_attn_wq"].transpose(1, 0, 2).reshape(D, P),
        "wk": v["L0_attn_wk"].transpose(1, 0, 2).reshape(D, P),
        "wv": v["L0_attn_wv"].transpose(1, 0, 2).reshape(D, P),
        "bq": v["L0_attn_bq"].reshape(P, 1),
        "bk": v["L0_attn_bk"].reshape(P, 1),
        "bv": v["L0_attn_bv"].reshape(P),
        "vectors": np.stack([v["L0_attn_bo"], v["L1_attn_bo"], v["L1_ffn_gamma"], v["L1_ffn_beta"]]),
        "wo": v["L0_attn_wo"].T,
        "gate_w": v["L0_ffn_gate_w"].T,
        "w1_0": v["L0_ffn_w1"],
        "w2_0": v["L0_ffn_w2"],
        "w1_1": v["L1_ffn_W1"],
        "w2_1": v["L1_ffn_W2"],
        "b1": v["L1_ffn_b1"].reshape(E, NF, P).transpose(2, 0, 1),
        "b2": v["L1_ffn_b2"],
        "wq1": v["L1_attn_Wq"],
        "bq1": v["L1_attn_bq"].reshape(P, 1),
        "wd": v["L1_attn_Wd"],
        "bd": v["L1_attn_bd"].reshape(R, 1),
        "wu": np.concatenate([v["L1_attn_Wu"], v["L1_attn_bu"][None]]).reshape(R + 1, H, 2, HD)
                .transpose(0, 2, 1, 3).reshape(R + 1, 2 * D),
        "wo1": v["L1_attn_Wo"],
        "gate1": v["L1_ffn_gate_W"],
        "shared_w": v["L1_ffn_shared_W"],
        "shared_b": v["L1_ffn_shared_b"],
        "slots": np.arange(1, KSEL + 1, dtype=np.float32),
        "block_mask": np.concatenate([head[:, None] == head[None], head[:, None] == np.arange(H)[None]], 1
                                     ).astype(np.float32),
        "lower": (np.arange(E)[None] < np.arange(E)[:, None]).astype(np.float32),
    }


def kernel(**inputs):
    import numpy as np
    import concourse.bacc as bacc
    from concourse.bass_utils import run_bass_kernel_spmd

    arrays = {f"in_{name}": np.ascontiguousarray(a) for name, a in laid_out(
        {name: np.asarray(a) for name, a in inputs.items()}).items()}
    nc = bacc.Bacc("TRN2", target_bir_lowering=False, num_devices=1)
    io = {name[3:]: nc.dram_tensor(name, a.shape, mybir.dt.from_np(a.dtype), kind="ExternalInput").ap()
          for name, a in arrays.items()}
    io["out"] = nc.dram_tensor("out_x", (B, T, D), F32, kind="ExternalOutput").ap()
    build(nc, io)
    result = run_bass_kernel_spmd(nc, [arrays], core_ids=[0])
    return result.results[0]["out_x"]
```
